# Optimizing a Trainium2 kernel written in Bass

```python
import numpy as np
import jax
import jax.numpy as jnp

def _softmax(x, axis=-1):
    return jax.nn.softmax(x, axis=axis)

def _gelu(x):
    return jax.nn.gelu(x, approximate=True)

def _silu(x):
    return jax.nn.silu(x)

def _sigmoid(x):
    return jax.nn.sigmoid(x)

def _layernorm(x, axis=-1, eps=1e-05):
    m = jnp.mean(x, axis=axis, keepdims=True)
    v = jnp.var(x, axis=axis, keepdims=True)
    return (x - m) / jnp.sqrt(v + eps)

def _scatter_add(tgt, idx, src, axis=0):
    return tgt.at[idx].add(src)

def _segment_sum(src, seg, n):
    return jax.ops.segment_sum(src, seg, n)
kernel_name = 'mk_adaln_d1_jaxref_r8_b84751'

def setup_inputs(seed: int=0):
    np.random.seed(seed)
    _w = jnp.asarray

    def _L0_attn_setup():
        import jax, jax.numpy as jnp
        import numpy as np
        import math
        D_MODEL = 128
        NHEAD = 16
        M = 32
        D_K = D_MODEL // NHEAD
        EPS = 1e-06

        def create_orf(key, d_k, m):
            k1, k2 = jax.random.split(key)
            n_blocks = math.ceil(m / d_k)
            blocks = jax.random.normal(k1, (n_blocks, d_k, d_k), dtype=jnp.float32)
            q, _ = jnp.linalg.qr(blocks)
            scale = jnp.linalg.norm(jax.random.normal(k2, (m, d_k), dtype=jnp.float32), axis=1)
            return scale[:, None] * q.reshape(-1, d_k)[:m]

        def feature_map(x, orf):
            m, d_k = orf.shape
            proj = x @ orf.T / d_k ** 0.25
            norm = jnp.sum(x * x, axis=-1, keepdims=True) / (2.0 * math.sqrt(d_k))
            return (jnp.exp(proj - norm) + EPS) / math.sqrt(m)
        key = jax.random.key(seed)
        ks = jax.random.split(key, 10)
        s = 1.0 / math.sqrt(D_MODEL)
        inp = {'x': jax.random.normal(ks[0], (4, 512, D_MODEL), dtype=jnp.float32)}
        names = ['q', 'k', 'v', 'o']
        for i, n in enumerate(names):
            inp[f'W{n}'] = jax.random.uniform(ks[1 + 2 * i], (D_MODEL, D_MODEL), dtype=jnp.float32, minval=-s, maxval=s)
            inp[f'b{n}'] = jax.random.uniform(ks[2 + 2 * i], (D_MODEL,), dtype=jnp.float32, minval=-s, maxval=s)
        inp['orf'] = create_orf(ks[9], D_K, M)
        return inp
    _L0_attn_in = _L0_attn_setup()

    def _L0_ffn_setup():
        import jax, jax.numpy as jnp
        import numpy as np
        B, T, D, DFF, E = (4, 256, 128, 512, 8)
        key = jax.random.key(seed)
        ks = jax.random.split(key, 4)
        s_in = 1.0 / np.sqrt(D)
        s_ff = 1.0 / np.sqrt(DFF)
        return {'x': jax.random.normal(ks[0], (B, T, D), dtype=jnp.float32), 'gate_W': jax.random.normal(ks[1], (D, E), dtype=jnp.float32) * s_in, 'gate_b': jnp.zeros((E,), dtype=jnp.float32), 'W1': jax.random.normal(ks[2], (E, D, DFF), dtype=jnp.float32) * s_in, 'b1': jnp.zeros((E, DFF), dtype=jnp.float32), 'W2': jax.random.normal(ks[3], (E, DFF, D), dtype=jnp.float32) * s_ff, 'b2': jnp.zeros((E, D), dtype=jnp.float32)}
    _L0_ffn_in = _L0_ffn_setup()
    _L0_c = _w((lambda *s: np.random.randn(*s).astype(np.float32) * 0.05)(16, 128))
    _L0_wmod = _w((lambda *s: np.random.randn(*s).astype(np.float32) * 0.05)(128, 6 * 128) * 128 ** (-0.5))
    _d = {'L0_attn_x': _L0_attn_in['x'], 'L0_attn_Wq': _L0_attn_in['Wq'], 'L0_attn_bq': _L0_attn_in['bq'], 'L0_attn_Wk': _L0_attn_in['Wk'], 'L0_attn_bk': _L0_attn_in['bk'], 'L0_attn_Wv': _L0_attn_in['Wv'], 'L0_attn_bv': _L0_attn_in['bv'], 'L0_attn_Wo': _L0_attn_in['Wo'], 'L0_attn_bo': _L0_attn_in['bo'], 'L0_attn_orf': _L0_attn_in['orf'], 'L0_ffn_gate_W': _L0_ffn_in['gate_W'], 'L0_ffn_gate_b': _L0_ffn_in['gate_b'], 'L0_ffn_W1': _L0_ffn_in['W1'], 'L0_ffn_b1': _L0_ffn_in['b1'], 'L0_ffn_W2': _L0_ffn_in['W2'], 'L0_ffn_b2': _L0_ffn_in['b2'], 'L0_c': _L0_c, 'L0_wmod': _L0_wmod}
    _x0 = _d['L0_attn_x']
    _d['L0_attn_x'] = jax.random.normal(jax.random.fold_in(jax.random.key(seed), 1), (16, 512, 128), dtype=_x0.dtype)
    del _x0
    return _d

def reference(L0_attn_x, L0_attn_Wq, L0_attn_bq, L0_attn_Wk, L0_attn_bk, L0_attn_Wv, L0_attn_bv, L0_attn_Wo, L0_attn_bo, L0_attn_orf, L0_ffn_gate_W, L0_ffn_gate_b, L0_ffn_W1, L0_ffn_b1, L0_ffn_W2, L0_ffn_b2, L0_c, L0_wmod):

    def _L0_attn_ref(x, Wq, bq, Wk, bk, Wv, bv, Wo, bo, orf):
        import jax, jax.numpy as jnp
        import numpy as np
        import math
        D_MODEL = 128
        NHEAD = 16
        M = 32
        D_K = D_MODEL // NHEAD
        EPS = 1e-06

        def create_orf(key, d_k, m):
            k1, k2 = jax.random.split(key)
            n_blocks = math.ceil(m / d_k)
            blocks = jax.random.normal(k1, (n_blocks, d_k, d_k), dtype=jnp.float32)
            q, _ = jnp.linalg.qr(blocks)
            scale = jnp.linalg.norm(jax.random.normal(k2, (m, d_k), dtype=jnp.float32), axis=1)
            return scale[:, None] * q.reshape(-1, d_k)[:m]

        def feature_map(x, orf):
            m, d_k = orf.shape
            proj = x @ orf.T / d_k ** 0.25
            norm = jnp.sum(x * x, axis=-1, keepdims=True) / (2.0 * math.sqrt(d_k))
            return (jnp.exp(proj - norm) + EPS) / math.sqrt(m)
        B, L, D = x.shape
        H, dh = (NHEAD, D // NHEAD)

        def split(y):
            return y.reshape(B, L, H, dh).transpose(0, 2, 1, 3).reshape(B * H, L, dh)
        q = feature_map(split(x @ Wq.T + bq), orf)
        k = feature_map(split(x @ Wk.T + bk), orf)
        v = split(x @ Wv.T + bv)
        kv = jnp.einsum('nlm,nld->nmd', k, v)
        ksum = jnp.sum(k, axis=1)
        buf = jnp.concatenate([kv, ksum[..., None]], axis=-1)
        out = jnp.einsum('nlm,nmd->nld', q, buf)
        out = out[..., :-1] / out[..., -1:]
        out = out.reshape(B, H, L, dh).transpose(0, 2, 1, 3).reshape(B, L, D)
        return out @ Wo.T + bo

    def _L0_ffn_ref(x, gate_W, gate_b, W1, b1, W2, b2):
        import jax, jax.numpy as jnp
        import numpy as np
        B, T, D, DFF, E = (4, 256, 128, 512, 8)
        b, t, d = x.shape
        num_experts = gate_W.shape[-1]
        logits = jnp.einsum('btd,de->bte', x, gate_W) + gate_b
        top1 = jnp.argmax(logits, axis=-1).reshape(-1)
        flat_x = x.reshape(b * t, d)
        out = jnp.zeros_like(flat_x)
        for e in range(num_experts):
            mask = (top1 == e).astype(x.dtype)[:, None]
            h = jax.nn.gelu(flat_x * mask @ W1[e] + b1[e], approximate=False)
            out = out + (h @ W2[e] + b2[e]) * mask
        return out.reshape(b, t, d)
    x = L0_attn_x
    mod = (_silu(L0_c) @ L0_wmod).reshape(L0_c.shape[0], 6, 1, -1)
    sa, ca, ga, sb, cb, gb = (mod[:, 0], mod[:, 1], mod[:, 2], mod[:, 3], mod[:, 4], mod[:, 5])
    ga = (2 * (ga >= 0) - 1) * jnp.maximum(jnp.abs(ga), 0.25)
    gb = (2 * (gb >= 0) - 1) * jnp.maximum(jnp.abs(gb), 0.25)
    h = _layernorm(x, axis=-1) * (1 + ca) + sa
    x = x + ga * _L0_attn_ref(h, L0_attn_Wq, L0_attn_bq, L0_attn_Wk, L0_attn_bk, L0_attn_Wv, L0_attn_bv, L0_attn_Wo, L0_attn_bo, L0_attn_orf)
    h = _layernorm(x, axis=-1) * (1 + cb) + sb
    x = x + gb * _L0_ffn_ref(h, L0_ffn_gate_W, L0_ffn_gate_b, L0_ffn_W1, L0_ffn_b1, L0_ffn_W2, L0_ffn_b2)
    return x

_drawn_inputs = setup_inputs


def setup_inputs(seed=0):
    import zlib

    import numpy as np

    out = dict(_drawn_inputs(seed))
    spreads = {'L0_ffn_gate_b': (0.0, 0.1), 'L0_ffn_b1': (0.0, 0.1), 'L0_ffn_b2': (0.0, 0.1)}
    factors = {}
    for name, (base, spread) in spreads.items():
        noise = np.random.default_rng([zlib.crc32(name.encode()), seed]).standard_normal(out[name].shape)
        drawn = base * np.exp(spread * noise) if base else spread * noise
        out[name] = jnp.asarray(drawn.astype(out[name].dtype))
    for name, factor in factors.items():
        out[name] = (out[name] * factor).astype(out[name].dtype)
    return out
```

```python
from contextlib import ExitStack

import numpy as np

import concourse.bass as bass
from concourse import mybir

F32 = mybir.dt.float32
BF16 = mybir.dt.bfloat16
I32 = mybir.dt.int32
ACT = mybir.ActivationFunctionType
ALU = mybir.AluOpType
AX = mybir.AxisListType

B, L, D = 16, 512, 128
NH, DH, M = 16, 8, 32
E, DFF = 8, 512
P = 128
LT = L // P
NT = B * LT
NC = NH * M // P
CW = NC and D // NC
FC = DFF // P
NBLK = NT + E
U = 4
FEPS = 1e-6
LNEPS = 1e-5
GMIN = 0.25
KP = P + 2
ROWS = 4
GA, SB, CB, GB = range(ROWS)

W_QA, W_QB, W_KA, W_KB, W_V, W_O = (i * P for i in range(6))
W_ORF = 6 * P
W_GATE = W_ORF + 2 * P
W_BIAS = W_GATE + CW
W_B1 = W_BIAS + 4
W_CT = W_B1 + E * FC
W_END = W_CT + B
C_ID, C_MASK, C_TRI, C_NORM = 0, P, 2 * P, 3 * P
C_SCAN = C_NORM + 2 * P
C_PREF = C_SCAN + NT * E
C_BLK = C_PREF + E
C_END = C_BLK + NBLK
R_BV, R_BO, R_GB, R_B2 = 0, D, 2 * D, 2 * D + E
R_END = R_B2 + E * D


class Steps:

    def __init__(self, eng, sem, base):
        self.eng, self.sem, self.base, self.n = eng, sem, base, 0

    def mark(self, instruction):
        instruction.then_inc(self.sem, 1)
        self.n += 1

    def wait(self):
        self.eng.wait_ge(self.sem, self.base + self.n)


def build(nc, x, weights, consts, rows, wmod, w1, w2, out):
    xs = nc.dram_tensor("sorted_tokens", [NBLK * P, D], F32).ap()
    ys = nc.dram_tensor("sorted_results", [NBLK * P, D], F32).ap()
    mods = nc.dram_tensor("modulation_rows", [B, ROWS * D], F32).ap()

    with ExitStack() as ctx:
        def sb(name, shape, dt=F32):
            return ctx.enter_context(nc.sbuf_tensor(name, shape, dt))

        def pb(name):
            return ctx.enter_context(nc.psum_tensor(name, [P, 512], F32))

        def sem(name):
            return ctx.enter_context(nc.semaphore(name))

        xall = sb("xall", [P, NT, D])
        h2all = sb("h2all", [P, NT, D])
        modb = sb("modb", [P, B, ROWS, D])
        wsb = sb("wsb", [P, W_END])
        csb = sb("csb", [P, C_END])
        rsb = sb("rsb", [P, R_END])
        w1sb = sb("w1sb", [P, E * DFF])
        w2sb = sb("w2sb", [P, E * DFF])
        feat_w = sb("feat_w", [P, 2 * P])
        ones32 = sb("ones32", [P, CW])
        mhalf = sb("mhalf", [P, LT])
        zeros = sb("zeros", [P, 9 * D])
        wmod_sb = h2all[:, 0:6, :].rearrange("p a b -> p (a b)")
        silu = sb("silu", [P, 3, B])
        modrow = sb("modrow", [B, ROWS, D])
        gsign = sb("gsign", [B, 2, D])
        ca1 = sb("ca1", [P, B])
        sa = sb("sa", [P, B])
        st1 = sb("st1", [P, LT, 6])
        mv1 = sb("mv1", [P, LT, 3])
        ve1 = sb("ve1", [P, LT])
        rstd1 = sb("rstd1", [P, LT])
        st2 = sb("st2", [P, LT, 6])
        mv2 = sb("mv2", [P, LT, 3])
        ve2 = sb("ve2", [P, LT])
        rstd2 = sb("rstd2", [P, LT])
        xn1 = sb("xn1", [P, LT, D])
        xn2 = sb("xn2", [P, LT, D])
        hT = sb("hT", [P, L])
        stack = [sb(f"stack{i}", [P, L]) for i in range(4)]
        v_sb = sb("v_sb", [P, LT, D])
        kf = sb("kf", [P, LT, NC, KP])
        qf = sb("qf", [P, NC, L])
        kvT = sb("kvT", [P, 2 * P])
        kvsum = sb("kvsum", [P, 2])
        kveps = sb("kveps", [P, 2])
        kvm = sb("kvm", [P, 2 * P])
        den = sb("den", [P, L])
        rden = sb("rden", [P, L])
        oT = sb("oT", [P, L])
        wo = sb("wo", [P, D])
        bog = sb("bog", [P, D])
        h2 = sb("h2", [P, LT, D])
        h2T = sb("h2T", [P, L])
        lgT = sb("lgT", [P, P])
        lg = sb("lg", [P, NT, E])
        tri = sb("tri", [P, P], BF16)
        ones_bf = sb("ones_bf", [P, P], BF16)
        top = sb("top", [P, NT])
        rt = [r[:, :].rearrange("p (e t) -> p e t", e=E) for r in (hT, den, rden)]
        oh = sb("oh", [P, E, NT], BF16)
        cnt_f = sb("cnt_f", [P, E])
        cnt_i = sb("cnt_i", [P, E], I32)
        nblk = sb("nblk", [P, E])
        endblk = sb("endblk", [P, E])
        base = sb("base", [P, E])
        slot_f = sb("slot_f", [P, NT])
        slot = sb("slot", [P, NT], I32)
        blk_ge = qf[:, 0:2, :].rearrange("p c l -> p (c l)")[:, 0:NBLK * E].rearrange("p (b e) -> p b e", e=E)
        blk_f = sb("blk_f", [P, NBLK])
        blk_e = sb("blk_e", [P, NBLK], I32)
        xin = [sb(f"xin{u}", [P, D]) for u in range(U)]
        xT = [sb(f"xT{u}", [P, P]) for u in range(2)]
        w1c = [stack[0], stack[1]]
        g = [qf[:, u, :] for u in range(U)]
        yb = [sb(f"yb{u}", [P, D]) for u in range(2)]

        F = [pb("ps_feat0"), pb("ps_feat1")]
        KV, G = pb("ps_kv"), pb("ps_den")
        H, I = pb("ps_out"), pb("ps_gate")
        PJ = [pb("ps_proj0"), pb("ps_proj1")]
        HID = [F[0], F[1], KV, G]
        XT = [H, I]
        Y = PJ

        ident = csb[:, C_ID:C_ID + P]
        mask = csb[:, C_MASK:C_MASK + P]

        s_w = sem("weights_in")
        s_c = sem("consts_in")
        s_r = sem("rows_in")
        s_wm = sem("wmod_in")
        s_w1 = sem("w1_in")
        s_w2 = sem("w2_in")
        s_x = [sem("x_in_even"), sem("x_in_odd")]
        s_mrow = sem("mod_rows_out")
        s_mb = sem("mod_rows_in")
        s_set = sem("setup_step")
        s_pset = sem("pool_setup")
        s_fw = sem("feature_weights")
        s_silue = sem("silu_exp")
        s_silu = sem("silu_ready")
        s_modp = sem("mod_products")
        s_modr = sem("mod_rows_ready")
        s_cols = sem("mod_columns_ready")
        s_zero = sem("sorted_zeroed")
        s_ln1 = sem("ln1_step")
        s_ln2 = sem("ln2_step")
        s_var1 = sem("var1_ready")
        s_var2 = sem("var2_ready")
        s_rstd1 = sem("rstd1_ready")
        s_rstd2 = sem("rstd2_ready")
        s_xn1 = sem("xn1_ready")
        s_xn2 = sem("xn2_ready")
        s_t1 = sem("xn1_transposed")
        s_hT = sem("hT_ready")
        s_proj = sem("projections")
        s_cp = sem("stack_values")
        s_sq = sem("stack_squares")
        s_v = sem("v_ready")
        s_feat = sem("feature_products")
        s_exp = sem("features_ready")
        s_kv = sem("kv_product")
        s_kvs = sem("kv_step")
        s_kvT = sem("kvT_ready")
        s_kvt = sem("kv_transposed")
        s_kvm = sem("kvm_ready")
        s_eps = sem("kveps_ready")
        s_den = sem("den_product")
        s_num = sem("num_product")
        s_denp = sem("den_ready")
        s_rden = sem("rden_ready")
        s_oT = sem("oT_ready")
        s_wo = sem("wo_ready")
        s_bog = sem("bog_ready")
        s_xb = sem("xb_ready")
        s_op = sem("out_product")
        s_x2 = sem("x2_ready")
        s_h2m = sem("h2_scaled")
        s_h2 = sem("h2_ready")
        s_h2t = sem("h2_transposed")
        s_h2T = sem("h2T_ready")
        s_h2c = sem("h2_kept")
        s_lg = sem("gate_product")
        s_lgT = sem("gateT_ready")
        s_lgt = sem("gate_transposed")
        s_lgs = sem("logits_ready")
        s_rt = sem("routing_step")
        s_oh = sem("onehot_ready")
        s_cnt = sem("count_products")
        s_slot = sem("slots_ready")
        s_blk = sem("block_table_ready")
        s_scat = sem("tokens_scattered")
        s_xin = [sem(f"block_in{u}") for u in range(U)]
        s_bt = sem("block_transposed")
        s_bT = sem("block_T_ready")
        s_w1c = sem("w1_copied")
        s_hid = sem("hidden_product")
        s_gelu = sem("hidden_ready")
        s_y = sem("result_product")
        s_yb = sem("result_ready")
        s_yout = [sem("result_out0"), sem("result_out1")]
        s_gath = [sem("gathered_even"), sem("gathered_odd")]
        s_fin = sem("final_step")
        s_scaled = sem("results_scaled")
        s_outr = sem("out_ready")
        s_out = sem("out_stored")

        block = ctx.enter_context(nc.Block())

        def apart(eng):
            eng.wait_ge(s_w, 16)

        def snapped(eng, value):
            return value if isinstance(value, int) else eng.snap(value)

        @block.sync
        def _(sp):
            sp.dma_start(wsb[:], weights).then_inc(s_w, 16)
            sp.dma_start(wmod_sb, wmod).then_inc(s_wm, 16)
            sp.dma_start(csb[:], consts).then_inc(s_c, 16)
            xv = x.rearrange("b (p t) d -> b p t d", t=LT)

            def load_x(b, parity):
                sp.dma_start(xall[:, bass.ds(b * LT, LT), :], xv[bass.ds(b, 1), :, :, :])\
                    .then_inc(s_x[parity], 16)

            load_x(0, 0)
            load_x(1, 1)
            sp.dma_start(rsb[:], rows).then_inc(s_r, 16)
            sp.wait_ge(s_modr, 1)
            sp.dma_start(mods, modrow[:, :, :].rearrange("b r d -> b (r d)")).then_inc(s_mrow, 16)
            sp.wait_ge(s_mrow, 16)
            sp.dma_start(modb[:, :, :, :].rearrange("p b r d -> p (b r d)"),
                         mods.rearrange("b n -> (b n)").unsqueeze(0).to_broadcast([P, B * ROWS * D]))\
                .then_inc(s_mb, 16)
            with sp.Fori(1, B // 2) as i:
                for parity in range(2):
                    sp.wait_ge(s_x[parity], 16 * i)
                    load_x(2 * i + parity, parity)
            sp.wait_ge(s_pset, 2)
            xz = xs.rearrange("(n p r) d -> n p (r d)", p=P, r=9)
            for n in range(NBLK // 9):
                sp.dma_start(xz[n], zeros[:]).then_inc(s_zero, 16)
            sp.dma_start(w1sb[:, :].rearrange("p (e f) -> p e f", e=E), w1.rearrange("e d f -> d e f"))\
                .then_inc(s_w1, 16)
            sp.dma_start(w2sb[:, :].rearrange("p (e c d) -> p e c d", e=E, c=FC),
                         w2.rearrange("e (c p) d -> p e c d", p=P)).then_inc(s_w2, 16)

            xb = xs.rearrange("(n p) d -> n p d", p=P)
            yo = ys.rearrange("(n p) d -> n p d", p=P)

            def load_block(k, u):
                sp.dma_start(xin[u][:], xb[bass.ds(k, 1), :, :].squeeze(0)).then_inc(s_xin[u], 16)

            def store_block(k, u):
                sp.wait_ge(s_yb, k + 1)
                sp.dma_start(yo[bass.ds(k, 1), :, :].squeeze(0), yb[u % 2][:])\
                    .then_inc(s_yout[u % 2], 16)

            sp.wait_ge(s_scat, 16 * NT)
            for u in range(U):
                load_block(u, u)

            def turn(i, first=False, last=False):
                for u in range(U):
                    k = i * U + u
                    if not (first and u < 2):
                        store_block(k - 2, u)
                    if not last:
                        sp.wait_ge(s_bt, k + 1)
                        load_block(k + U, u)

            turn(0, first=True)
            with sp.Fori(1, NBLK // U - 1) as i:
                turn(i)
            turn(NBLK // U - 1, last=True)
            for u in range(2):
                store_block(NBLK - 2 + u, u)

            ov = out.rearrange("b (p t) d -> b p t d", t=LT)
            with sp.Fori(0, B) as b:
                sp.wait_ge(s_outr, b + 1)
                sp.dma_start(ov[bass.ds(b, 1), :, :, :], xall[:, bass.ds(b * LT, LT), :])\
                    .then_inc(s_out, 16)
            sp.wait_ge(s_out, 16 * B)

        @block.gpsimd
        def _(pool):
            g_ = nc.gpsimd
            g_.memset(zeros[:], 0.0).then_inc(s_pset, 1)
            g_.memset(mhalf[:], -0.5).then_inc(s_pset, 1)
            pool.wait_ge(s_pset, 2)

            def rstd(b, which):
                ve, out_, ready, done = ((ve1, rstd1, s_var1, s_rstd1), (ve2, rstd2, s_var2, s_rstd2))[which]
                pool.wait_ge(ready, b + 1)
                g_.tensor_tensor(out_[:], ve[:], mhalf[:], ALU.pow).then_inc(done, 1)

            def gated(b, first=False):
                if not first:
                    apart(pool)
                    pool.wait_ge(s_op, b)
                g_.tensor_tensor(wo[:], wsb[:, W_O:W_O + D], modb[:, bass.ds(b, 1), GA, :].squeeze(1), ALU.mult).then_inc(s_wo, 1)
                if not first:
                    apart(pool)
                    pool.wait_ge(s_xb, b)
                g_.tensor_tensor(bog[:], rsb[:, R_BO:R_BO + D], modb[:, bass.ds(b, 1), GA, :].squeeze(1), ALU.mult).then_inc(s_bog, 1)
                apart(pool)
                pool.wait_ge(s_bog, b + 1)
                pool.wait_ge(s_xn1, b + 1)
                xt = xall[:, bass.ds(b * LT, LT), :]
                g_.tensor_tensor(xt, xt, bog[:, :].unsqueeze(1).to_broadcast([P, LT, D]), ALU.add)\
                    .then_inc(s_xb, 1)

            def experts_input(b):
                apart(pool)
                pool.wait_ge(s_xn2, b + 1)
                g_.tensor_tensor(h2[:], xn2[:], modb[:, bass.ds(b, 1), CB, :].to_broadcast([P, LT, D]), ALU.mult)\
                    .then_inc(s_h2m, 1)
                apart(pool)
                pool.wait_ge(s_h2m, b + 1)
                g_.tensor_tensor(h2[:], h2[:], modb[:, bass.ds(b, 1), SB, :].to_broadcast([P, LT, D]), ALU.add)\
                    .then_inc(s_h2, 1)

            rstd(0, 0)
            rstd(1, 0)
            pool.wait_ge(s_r, 16)
            pool.wait_ge(s_mb, 16)
            gated(0, first=True)
            with pool.Fori(1, B - 1) as b:
                rstd(b - 1, 1)
                rstd(b + 1, 0)
                experts_input(b - 1)
                gated(b)
            rstd(B - 2, 1)
            experts_input(B - 2)
            gated(B - 1)
            rstd(B - 1, 1)
            experts_input(B - 1)

            pool.wait_ge(s_zero, 16 * (NBLK // 9))
            pool.wait_ge(s_slot, 1)
            pool.wait_ge(s_h2c, B)
            for t in range(NT):
                g_.indirect_dma_start(out=xs, out_offset=bass.IndirectOffsetOnAxis(ap=slot[:, t:t + 1], axis=0),
                                      in_=h2all[:, t, :], in_offset=None).then_inc(s_scat, 16)
            for par in range(2):
                pool.wait_ge(s_yout[par], 16 * (NBLK // 2))
            for t in range(NT):
                bpar = (t // LT) % 2
                if t >= 2 * LT and t % LT == 0:
                    pool.wait_ge(s_gath[bpar], 16 * LT * (t // LT // 2))
                g_.indirect_dma_start(out=h2all[:, t, :], out_offset=None, in_=ys,
                                      in_offset=bass.IndirectOffsetOnAxis(ap=slot[:, t:t + 1], axis=0))\
                    .then_inc(s_gath[bpar], 16)

        @block.scalar
        def _(act):
            a = nc.scalar
            act.wait_ge(s_w, 16)
            a.activation(silu[:, 0, :], wsb[:, W_CT:W_CT + B], ACT.Exp, scale=-1.0).then_inc(s_silue, 1)

            def squares(b, i, first=False):
                act.wait_ge(s_proj, 5 * b + i + 1)
                a.activation(stack[i][64:128, :], PJ[i % 2][64:128, :], ACT.Square,
                             bias=wsb[64:128, W_BIAS + i:W_BIAS + i + 1]).then_inc(s_sq, 1)

            def feature(b, j):
                act.wait_ge(s_feat, 2 * NC * b + j + 1)
                src = F[j % 2][:, :]
                if j < LT:
                    dst, src = kf[:, j, :, 0:P], src.rearrange("p (c m) -> p c m", c=NC)
                else:
                    dst = qf[:, j - LT, :]
                a.activation(dst, src, ACT.Exp).then_inc(s_exp, 1)

            def keep_h2(b):
                a.activation(h2all[:, bass.ds(b * LT, LT), :], h2[:], ACT.Copy).then_inc(s_h2c, 1)

            def batch(b, first=False, last=False):
                for j in range(2 * NC):
                    feature(b, j)
                if not first:
                    act.wait_ge(s_h2t, b)
                    a.activation(h2T[:], I[:], ACT.Copy).then_inc(s_h2T, 1)
                    keep_h2(b - 1)
                act.wait_ge(s_kvt, b + 1)
                a.activation(kvm[:], G[:, 0:2 * P], ACT.Copy).then_inc(s_kvm, 1)
                if not last:
                    squares(b + 1, 0)
                    squares(b + 1, 1)
                act.wait_ge(s_den, b + 1)
                act.wait_ge(s_eps, b + 1)
                a.activation(den[:], G[:], ACT.Identity, bias=kveps[:, 1:2]).then_inc(s_denp, 1)
                if not last:
                    squares(b + 1, 2)
                    squares(b + 1, 3)

            for i in range(4):
                squares(0, i)
            batch(0, first=True)
            with act.Fori(1, B - 1) as b:
                batch(b)
            batch(B - 1, last=True)
            act.wait_ge(s_h2t, B)
            a.activation(h2T[:], I[:], ACT.Copy).then_inc(s_h2T, 1)
            keep_h2(B - 1)

            act.wait_ge(s_blk, 1)
            with act.Fori(0, NBLK // U) as i:
                for u in range(U):
                    e = act.value_load(blk_e[0:1, bass.ds(i * U + u, 1)], min_val=0, max_val=E - 1)
                    act.wait_ge(s_hid, i * U + u + 1)
                    for c in range(FC):
                        ins = a.activation(g[u][:, c * P:(c + 1) * P], HID[u][:, c * P:(c + 1) * P], ACT.Gelu,
                                           bias=wsb[:, bass.ds(e * FC + (W_B1 + c), 1)])
                    ins.then_inc(s_gelu, 1)

        @block.vector
        def _(dve):
            v = nc.vector

            v.memset(ones32[:], 1.0).then_inc(s_set, 1)
            v.memset(kf[:, :, :, P:KP], FEPS).then_inc(s_set, 1)
            v.memset(ones_bf[:], 1.0).then_inc(s_set, 1)
            dve.wait_ge(s_silue, 1)
            v.tensor_scalar(silu[:, 1, :], silu[:, 0, :], 1.0, None, ALU.add).then_inc(s_set, 1)
            dve.wait_ge(s_set, 4)
            v.reciprocal(silu[:, 2, :], silu[:, 1, :]).then_inc(s_set, 1)
            dve.wait_ge(s_set, 5)
            v.tensor_tensor(silu[:, 0, :], silu[:, 2, :], wsb[:, W_CT:W_CT + B], ALU.mult).then_inc(s_silu, 1)
            dve.wait_ge(s_c, 16)
            v.scalar_tensor_tensor(out=feat_w[:], in0=wsb[:, W_ORF:W_ORF + 2 * P], scalar=float(DH ** -0.25),
                                   in1=csb[:, C_NORM:C_NORM + 2 * P], op0=ALU.mult, op1=ALU.add).then_inc(s_fw, 1)
            v.tensor_copy(tri[:], csb[:, C_TRI:C_TRI + P]).then_inc(s_fw, 1)
            dve.wait_ge(s_modp, 1)
            v.tensor_copy(sa[:], F[0][:, 0:B])
            v.tensor_scalar(ca1[:], F[0][:, B:2 * B], 1.0, None, ALU.add).then_inc(s_cols, 1)
            v.tensor_copy(modrow[:, SB, :], I[0:B, 0:D])
            v.tensor_scalar(modrow[:, CB, :], I[0:B, D:2 * D], 1.0, None, ALU.add)
            gates = [(n, row, src[0:B, 2 * D:3 * D]) for n, (row, src) in enumerate(((GA, H), (GB, I)))]
            for n, row, gate in gates:
                ins = v.tensor_scalar(gsign[:, n, :], gate, 0.0, 2.0, ALU.is_ge, ALU.mult)
            ins.then_inc(s_set, 1)
            dve.wait_ge(s_set, 6)
            v.tensor_scalar(gsign[:, :, :], gsign[:, :, :], -1.0, None, ALU.add).then_inc(s_set, 1)
            dve.wait_ge(s_set, 7)
            for n, row, gate in gates:
                ins = v.tensor_tensor(modrow[:, row, :], gate, gsign[:, n, :], ALU.mult)
            ins.then_inc(s_set, 1)
            dve.wait_ge(s_set, 8)
            for n, row, gate in gates:
                ins = v.scalar_tensor_tensor(out=modrow[:, row, :], in0=modrow[:, row, :], scalar=GMIN,
                                             in1=gsign[:, n, :], op0=ALU.max, op1=ALU.mult)
            ins.then_inc(s_modr, 1)

            def stats(b, which):
                st, mv, ve, step, ready = ((st1, mv1, ve1, s_ln1, s_var1), (st2, mv2, ve2, s_ln2, s_var2))[which]
                s = Steps(dve, step, 3 * b)
                for t in range(LT):
                    ins = v.bn_stats(st[:, t, :], xall[:, bass.ds(b * LT + t, 1), :].squeeze(1))
                s.mark(ins)
                s.wait()
                v.tensor_tensor(mv[:, :, 0:2], st[:, :, 1:3], st[:, :, 4:6], ALU.add)
                s.mark(v.tensor_tensor(mv[:, :, 2], st[:, :, 1], st[:, :, 4], ALU.subtract))
                s.wait()
                v.tensor_scalar(mv[:, :, 0], mv[:, :, 0], 0.5, None, ALU.mult)
                v.tensor_scalar(mv[:, :, 1], mv[:, :, 1], 1.0 / D, LNEPS, ALU.mult, ALU.add)
                s.mark(v.tensor_tensor(mv[:, :, 2], mv[:, :, 2], mv[:, :, 2], ALU.mult))
                s.wait()
                v.scalar_tensor_tensor(out=ve[:], in0=mv[:, :, 2], scalar=0.25, in1=mv[:, :, 1],
                                       op0=ALU.mult, op1=ALU.add).then_inc(ready, 1)

            def normalise(b, which, first=False):
                mv, rstd, xn, rdy, done = ((mv1, rstd1, xn1, s_rstd1, s_xn1), (mv2, rstd2, xn2, s_rstd2, s_xn2))[which]
                dve.wait_ge(rdy, b + 1)
                if not first:
                    dve.wait_ge(s_h2m if which else s_t1, b)
                for t in range(LT):
                    ins = v.tensor_scalar(xn[:, t, :], xall[:, bass.ds(b * LT + t, 1), :].squeeze(1), mv[:, t, 0:1],
                                          rstd[:, t:t + 1], ALU.subtract, ALU.mult)
                ins.then_inc(done, 1)

            def modulate(b):
                dve.wait_ge(s_t1, b + 1)
                v.tensor_scalar(hT[:], H[:], ca1[:, bass.ds(b, 1)], sa[:, bass.ds(b, 1)], ALU.mult, ALU.add)\
                    .then_inc(s_hT, 1)

            def values(b, i):
                dve.wait_ge(s_proj, 5 * b + i + 1)
                v.tensor_scalar(stack[i][0:64, :], PJ[i % 2][0:64, :], wsb[0:64, W_BIAS + i:W_BIAS + i + 1], None,
                                ALU.add).then_inc(s_cp, 1)

            def v_values(b):
                dve.wait_ge(s_proj, 5 * b + 5)
                v.tensor_tensor(v_sb[:], PJ[0][:, :].rearrange("p (t d) -> p t d", t=LT),
                                rsb[:, R_BV:R_BV + D].unsqueeze(1).to_broadcast([P, LT, D]), ALU.add).then_inc(s_v, 1)

            def kv_values(b, first=False):
                dve.wait_ge(s_kv, b + 1)
                if not first:
                    dve.wait_ge(s_denp, b)
                v.scalar_tensor_tensor(out=kvT[:, 0:P], in0=KV[:, 0:P], scalar=KV[:, P:P + 1], in1=mask,
                                       op0=ALU.add, op1=ALU.mult, accum_out=kvsum[:, 0:1])
                v.scalar_tensor_tensor(out=kvT[:, P:2 * P], in0=KV[:, 256:256 + P], scalar=float(L * FEPS), in1=mask,
                                       op0=ALU.add, op1=ALU.mult, accum_out=kvsum[:, 1:2]).then_inc(s_kvT, 1)
                dve.wait_ge(s_kvT, b + 1)
                v.tensor_scalar(kveps[:], kvsum[:], FEPS, None, ALU.mult).then_inc(s_eps, 1)

            def attention(b):
                dve.wait_ge(s_denp, b + 1)
                v.reciprocal(rden[:], den[:]).then_inc(s_rden, 1)
                dve.wait_ge(s_rden, b + 1)
                dve.wait_ge(s_num, b + 1)
                v.scalar_tensor_tensor(out=oT[:], in0=KV[:], scalar=kveps[:, 0:1], in1=rden[:],
                                       op0=ALU.add, op1=ALU.mult).then_inc(s_oT, 1)

            def residual(b):
                dve.wait_ge(s_op, b + 1)
                dve.wait_ge(s_xb, b + 1)
                xt = xall[:, bass.ds(b * LT, LT), :]
                v.tensor_tensor(xt, H[:, :].rearrange("p (t d) -> p t d", t=LT), xt, ALU.add).then_inc(s_x2, 1)
                value = snapped(dve, b + 1)
                apart(dve)
                dve.wait_ge(s_x2, value)

            def gateT(b):
                dve.wait_ge(s_lg, b + 1)
                v.tensor_copy(lgT[:], I[:, 0:P]).then_inc(s_lgT, 1)

            def logits(b):
                dve.wait_ge(s_lgt, b + 1)
                v.tensor_copy(lg[:, bass.ds(b * LT, LT), :],
                              I[:, P:2 * P].rearrange("p (t c) -> p t c", t=LT)[:, :, 0:E]).then_inc(s_lgs, 1)

            def batch(b, x_turn, first=False, last=False, parity=0):
                if not first:
                    residual(b - 1)
                    stats(b - 1, 1)
                if not last:
                    value = snapped(dve, 16 * x_turn)
                    apart(dve)
                    dve.wait_ge(s_x[parity], value)
                    stats(b + 1, 0)
                if not first:
                    normalise(b - 1, 1, first=isinstance(b, int) and b == 1)
                if not last:
                    normalise(b + 1, 0)
                    modulate(b + 1)
                kv_values(b, first)
                if not last:
                    values(b + 1, 0)
                    values(b + 1, 1)
                attention(b)
                if not last:
                    values(b + 1, 2)
                    values(b + 1, 3)
                    v_values(b + 1)
                if not first:
                    gateT(b - 1)
                    logits(b - 1)

            dve.wait_ge(s_x[0], 16)
            stats(0, 0)
            normalise(0, 0, first=True)
            dve.wait_ge(s_cols, 1)
            modulate(0)
            for i in range(4):
                values(0, i)
            dve.wait_ge(s_r, 16)
            v_values(0)
            batch(0, 1, first=True, parity=1)
            batch(1, 2, parity=0)
            with dve.Fori(1, B // 2 - 1) as i:
                batch(2 * i, i + 1, parity=1)
                batch(2 * i + 1, i + 2, parity=0)
            batch(B - 2, B // 2, parity=1)
            batch(B - 1, None, last=True)
            residual(B - 1)
            stats(B - 1, 1)
            normalise(B - 1, 1)
            gateT(B - 1)
            logits(B - 1)

            s = Steps(dve, s_rt, 0)

            def step(ins):
                s.mark(ins)
                s.wait()

            lgv = lg[:, :, :].rearrange("p t e -> p e t")
            te = [r.rearrange("p e t -> p t e") for r in rt]
            eb = lambda r: r.unsqueeze(1).to_broadcast([P, E, NT])
            tb = lambda r: r.unsqueeze(2).to_broadcast([P, E, NT])
            dve.wait_ge(s_lgs, B)
            step(v.tensor_tensor(rt[0], lgv, tb(rsb[:, R_GB:R_GB + E]), ALU.add))
            step(v.tensor_reduce(out=top[:], in_=te[0], op=ALU.max, axis=AX.X))
            step(v.tensor_tensor(rt[1], rt[0], eb(top[:, :]), ALU.is_ge))
            step(v.tensor_tensor(rt[2], rt[1], tb(csb[:, C_PREF:C_PREF + E]), ALU.mult))
            step(v.tensor_reduce(out=top[:], in_=te[2], op=ALU.max, axis=AX.X))
            v.tensor_tensor(oh[:], rt[2], eb(top[:, :]), ALU.is_equal).then_inc(s_oh, 1)
            dve.wait_ge(s_cnt, 1)
            step(v.tensor_copy(rt[0], F[1][:, :].rearrange("p (e t) -> p e t", e=E)))
            step(v.tensor_tensor_scan(out=rt[1].rearrange("p e t -> p (e t)"),
                                      data0=csb[:, C_SCAN:C_SCAN + NT * E],
                                      data1=rt[0].rearrange("p e t -> p (e t)"), initial=0.0,
                                      op0=ALU.mult, op1=ALU.add))
            step(v.tensor_scalar(cnt_f[:], rt[1][:, :, NT - 1], float(P - 1), None, ALU.add))
            step(v.tensor_copy(cnt_i[:], cnt_f[:]))
            step(v.tensor_scalar(cnt_i[:], cnt_i[:], P.bit_length() - 1, None, ALU.arith_shift_right))
            step(v.tensor_copy(nblk[:], cnt_i[:]))
            step(v.tensor_tensor_scan(out=endblk[:], data0=ones32[:, 0:E], data1=nblk[:], initial=0.0,
                                      op0=ALU.mult, op1=ALU.add))
            step(v.tensor_tensor(base[:], endblk[:], nblk[:], ALU.subtract))
            step(v.tensor_scalar(base[:], base[:], float(P), None, ALU.mult))
            step(v.tensor_tensor(rt[1], rt[1], rt[0], ALU.subtract))
            step(v.tensor_tensor(rt[1], F[0][:, :].rearrange("p (e t) -> p e t", e=E), rt[1], ALU.add))
            step(v.tensor_tensor(rt[1], rt[1], tb(base[:, :]), ALU.add))
            step(v.tensor_tensor(rt[2], rt[1], oh[:], ALU.mult))
            step(v.tensor_reduce(out=slot_f[:], in_=te[2], op=ALU.add, axis=AX.X))
            v.tensor_copy(slot[:], slot_f[:]).then_inc(s_slot, 1)
            step(v.tensor_tensor(blk_ge, csb[:, C_BLK:C_BLK + NBLK].unsqueeze(2).to_broadcast([P, NBLK, E]),
                                 endblk[:, :].unsqueeze(1).to_broadcast([P, NBLK, E]), ALU.is_ge))
            step(v.tensor_reduce(out=blk_f[:], in_=blk_ge, op=ALU.add, axis=AX.X))
            step(v.tensor_scalar(blk_f[:], blk_f[:], float(E - 1), None, ALU.min))
            v.tensor_copy(blk_e[:], blk_f[:]).then_inc(s_blk, 1)
            dve.wait_ge(s_blk, 1)
            dve.wait_ge(s_w1, 16)

            def expert_of(k):
                return dve.value_load(blk_e[0:1, bass.ds(k, 1)], min_val=0, max_val=E - 1)

            def copy_w1(k, u, first=False):
                e = expert_of(k)
                if not first:
                    apart(dve)
                    dve.wait_ge(s_hid, k - 1)
                v.tensor_copy(w1c[u % 2][:], w1sb[:, bass.ds(e * DFF, DFF)]).then_inc(s_w1c, 1)

            def copy_xT(k, u):
                dve.wait_ge(s_bt, k + 1)
                v.tensor_copy(xT[u % 2][:], XT[u % 2][:, 0:P]).then_inc(s_bT, 1)

            def turn(i, first=False, last=False):
                for u in range(U):
                    k = i * U + u
                    if not (last and u == U - 1):
                        copy_w1(k + 1, u + 1, first=first and u == 0)
                        copy_xT(k + 1, u + 1)
                    if not (first and u < 2):
                        e = expert_of(k - 2)
                        dve.wait_ge(s_y, k - 1)
                        if not (first and u < 4):
                            dve.wait_ge(s_yout[u % 2], 16 * (i * (U // 2) + u // 2 - 1))
                        v.tensor_tensor(yb[u % 2][:], Y[u % 2][:, 0:D],
                                        rsb[:, bass.ds(e * D + R_B2, D)], ALU.add).then_inc(s_yb, 1)

            copy_w1(0, 0, first=True)
            copy_xT(0, 0)
            turn(0, first=True)
            with dve.Fori(1, NBLK // U - 1) as i:
                turn(i)
            turn(NBLK // U - 1, last=True)
            for u in range(2):
                k = NBLK - 2 + u
                dve.wait_ge(s_y, k + 1)
                dve.wait_ge(s_yout[u], 16 * (k // 2))
                v.tensor_tensor(yb[u][:], Y[u][:, 0:D], rsb[:, bass.ds(expert_of(k) * D + R_B2, D)], ALU.add)\
                    .then_inc(s_yb, 1)

            def final(b, parity, gathers):
                ht = h2all[:, bass.ds(b * LT, LT), :]
                xt = xall[:, bass.ds(b * LT, LT), :]
                dve.wait_ge(s_gath[parity], 16 * LT * gathers)
                v.tensor_tensor(ht, ht, modb[:, bass.ds(b, 1), GB, :].to_broadcast([P, LT, D]), ALU.mult)\
                    .then_inc(s_scaled, 1)
                dve.wait_ge(s_scaled, b + 1)
                v.tensor_tensor(xt, xt, ht, ALU.add).then_inc(s_outr, 1)

            with dve.Fori(0, B // 2) as i:
                final(2 * i, 0, i + 1)
                final(2 * i + 1, 1, i + 1)

        @block.tensor
        def _(pe):
            mm, tr = nc.tensor.matmul, nc.tensor.transpose

            pe.wait_ge(s_silu, 1)
            pe.wait_ge(s_wm, 16)
            sc = silu[:, 0, :]
            mm(H[0:B, 0:3 * D], sc, wmod_sb[:, 0:3 * D], start=True, stop=True)
            mm(I[0:B, 0:3 * D], sc, wmod_sb[:, 3 * D:6 * D], start=True, stop=True)
            mm(F[0][:, 0:B], wmod_sb[:, 0:D], sc, start=True, stop=True)
            mm(F[0][:, B:2 * B], wmod_sb[:, D:2 * D], sc, start=True, stop=True).then_inc(s_modp, 1)

            def transpose_xn(b, first=False):
                pe.wait_ge(s_xn1, b + 1)
                if not first:
                    pe.wait_ge(s_x2, b - 1)
                for t in range(LT):
                    ins = tr(H[:, t * P:(t + 1) * P], xn1[:, t, :], ident)
                ins.then_inc(s_t1, 1)

            def project(b, i, first=False):
                if i == 0:
                    pe.wait_ge(s_hT, b + 1)
                    if not first:
                        pe.wait_ge(s_v, b)
                elif i == 1 and not first:
                    pe.wait_ge(s_cp, 4 * b)
                    pe.wait_ge(s_sq, 4 * b)
                elif i >= 2:
                    pe.wait_ge(s_cp, 4 * b + i - 1)
                    pe.wait_ge(s_sq, 4 * b + i - 1)
                if i < 4:
                    mm(PJ[i % 2][:, :], wsb[:, i * P:(i + 1) * P], hT[:], start=True, stop=True).then_inc(s_proj, 1)
                else:
                    for t in range(LT):
                        ins = mm(PJ[0][:, t * P:(t + 1) * P], hT[:, t * P:(t + 1) * P], wsb[:, W_V:W_V + D],
                                 start=True, stop=True)
                    ins.then_inc(s_proj, 1)

            def feature(b, j, first=False):
                if not (first and j < 2):
                    pe.wait_ge(s_exp, 2 * NC * b + j - 1)
                if j == 0:
                    pe.wait_ge(s_cp, 4 * b + 4)
                    pe.wait_ge(s_sq, 4 * b + 4)
                ps = F[j % 2]
                if j < LT:
                    for half in range(2):
                        ins = mm(ps[:, half * 2 * P:(half + 1) * 2 * P], stack[2 + half][:, j * P:(j + 1) * P],
                                 feat_w[:], start=True, stop=True)
                else:
                    c = j - LT
                    ins = mm(ps[:, :], feat_w[:, (c % 2) * P:(c % 2 + 1) * P], stack[c // 2][:], start=True, stop=True)
                ins.then_inc(s_feat, 1)

            def kv_product(b, first=False):
                pe.wait_ge(s_exp, 2 * NC * b + LT)
                pe.wait_ge(s_v, b + 1)
                if not first:
                    pe.wait_ge(s_oT, b)
                for t in range(LT):
                    for c in range(NC):
                        mm(KV[c * CW:(c + 1) * CW, 0:P + 1], v_sb[:, t, c * CW:(c + 1) * CW], kf[:, t, c, 0:P + 1],
                           start=(t == 0), stop=(t == LT - 1))
                for t in range(LT):
                    for c in range(NC):
                        ins = mm(KV[c * CW:(c + 1) * CW, 256:256 + P], ones32[:], kf[:, t, c, 0:P],
                                 start=(t == 0), stop=(t == LT - 1))
                ins.then_inc(s_kv, 1)

            def kv_transpose(b, first=False):
                pe.wait_ge(s_kvT, b + 1)
                for n in range(2):
                    ins = tr(G[:, n * P:(n + 1) * P], kvT[:, n * P:(n + 1) * P], ident)
                ins.then_inc(s_kvt, 1)

            def attend(b):
                pe.wait_ge(s_kvm, b + 1)
                pe.wait_ge(s_exp, 2 * NC * (b + 1))
                for c in range(NC):
                    ins = mm(G[c * CW:(c + 1) * CW, :], kvm[:, P + c * CW:P + (c + 1) * CW], qf[:, c, :],
                             start=True, stop=True)
                ins.then_inc(s_den, 1)
                for c in range(NC):
                    ins = mm(KV[c * CW:(c + 1) * CW, :], kvm[:, c * CW:(c + 1) * CW], qf[:, c, :],
                             start=True, stop=True)
                ins.then_inc(s_num, 1)

            def out_project(b, last=False):
                pe.wait_ge(s_oT, b + 1)
                pe.wait_ge(s_wo, b + 1)
                if not last:
                    pe.wait_ge(s_hT, b + 2)
                for t in range(LT):
                    ins = mm(H[:, t * P:(t + 1) * P], oT[:, t * P:(t + 1) * P], wo[:], start=True, stop=True)
                ins.then_inc(s_op, 1)

            def transpose_h2(b):
                pe.wait_ge(s_h2, b + 1)
                for t in range(LT):
                    ins = tr(I[:, t * P:(t + 1) * P], h2[:, t, :], ident)
                ins.then_inc(s_h2t, 1)

            def gate(b):
                pe.wait_ge(s_h2T, b + 1)
                for t in range(LT):
                    ins = mm(I[t * CW:(t + 1) * CW, 0:P], wsb[:, W_GATE:W_GATE + CW], h2T[:, t * P:(t + 1) * P],
                             start=True, stop=True)
                ins.then_inc(s_lg, 1)

            def gate_transpose(b):
                pe.wait_ge(s_lgT, b + 1)
                tr(I[:, P:2 * P], lgT[:], ident).then_inc(s_lgt, 1)

            def batch(b, first=False, last=False):
                for j in range(LT + 2):
                    feature(b, j, first)
                if not last:
                    transpose_xn(b + 1, first)
                kv_product(b, first)
                feature(b, LT + 2)
                feature(b, LT + 3)
                if not first:
                    transpose_h2(b - 1)
                kv_transpose(b, first)
                if not last:
                    project(b + 1, 0)
                    project(b + 1, 1)
                attend(b)
                if not last:
                    project(b + 1, 2)
                    project(b + 1, 3)
                    project(b + 1, 4)
                if not first:
                    gate(b - 1)
                out_project(b, last)
                if not first:
                    gate_transpose(b - 1)

            pe.wait_ge(s_modr, 1)
            pe.wait_ge(s_fw, 2)
            pe.wait_ge(s_set, 3)
            transpose_xn(0, first=True)
            for i in range(5):
                project(0, i, first=True)
            batch(0, first=True)
            with pe.Fori(1, B - 1) as b:
                batch(b)
            batch(B - 1, last=True)
            transpose_h2(B - 1)
            gate(B - 1)
            gate_transpose(B - 1)

            pe.wait_ge(s_oh, 1)
            ohv = oh[:, :, :].rearrange("p e t -> p (e t)")
            mm(F[0][:, :], tri[:], ohv, start=True, stop=True)
            mm(F[1][:, :], ones_bf[:], ohv, start=True, stop=True).then_inc(s_cnt, 1)
            pe.wait_ge(s_blk, 1)
            pe.wait_ge(s_w2, 16)

            def transpose_block(k, u, loads):
                pe.wait_ge(s_xin[u % U], 16 * loads)
                tr(XT[u % 2][:, 0:P], xin[u % U][:], ident).then_inc(s_bt, 1)

            def hidden(k, u):
                pe.wait_ge(s_w1c, k + 1)
                pe.wait_ge(s_bT, k + 1)
                for c in range(FC):
                    ins = mm(HID[u][:, c * P:(c + 1) * P], w1c[u % 2][:, c * P:(c + 1) * P], xT[u % 2][:],
                             start=True, stop=True)
                ins.then_inc(s_hid, 1)

            def second(k, u, early=False):
                e = pe.value_load(blk_e[0:1, bass.ds(k, 1)], min_val=0, max_val=E - 1)
                pe.wait_ge(s_gelu, k + 1)
                if not early:
                    pe.wait_ge(s_yb, k - 1)
                for c in range(FC):
                    ins = mm(Y[u % 2][:, 0:D], g[u][:, c * P:(c + 1) * P], w2sb[:, bass.ds(e * DFF + c * D, D)],
                             start=(c == 0), stop=(c == FC - 1))
                ins.then_inc(s_y, 1)

            def turn(i, first=False, last=False):
                for u in range(U):
                    k = i * U + u
                    if not (last and u == U - 1):
                        transpose_block(k + 1, u + 1, i + 1 + (u + 1) // U)
                    hidden(k, u)
                    if not (first and u < 2):
                        second(k - 2, (u - 2) % U, early=first)

            transpose_block(0, 0, 1)
            turn(0, first=True)
            with pe.Fori(1, NBLK // U - 1) as i:
                turn(i)
            turn(NBLK // U - 1, last=True)
            for u in range(2):
                second(NBLK - 2 + u, U - 2 + u)


def program(nc, ins, outs):
    build(nc, *ins, *outs)


_OUT = (B, L, D)


def _constants():
    c = np.zeros((P, C_END), np.float32)
    p = np.arange(P)
    c[:, C_ID:C_ID + P] = np.eye(P)
    c[:, C_MASK:C_MASK + P] = (p[:, None] % CW) // DH == p[None, :] // M
    c[:, C_TRI:C_TRI + P] = p[:, None] < p[None, :]
    for r in range(64):
        head = r // DH
        c[64 + r, C_NORM + head * M:C_NORM + (head + 1) * M] = -1.0 / (2.0 * DH ** 0.5)
    scan = np.ones((E, NT), np.float32)
    scan[:, 0] = 0.0
    c[:, C_SCAN:C_SCAN + NT * E] = scan.reshape(-1)
    c[:, C_PREF:C_PREF + E] = np.arange(E, 0, -1)
    c[:, C_BLK:C_BLK + NBLK] = np.arange(NBLK)
    return c


def kernel(L0_attn_x, L0_attn_Wq, L0_attn_bq, L0_attn_Wk, L0_attn_bk, L0_attn_Wv, L0_attn_bv, L0_attn_Wo,
           L0_attn_bo, L0_attn_orf, L0_ffn_gate_W, L0_ffn_gate_b, L0_ffn_W1, L0_ffn_b1, L0_ffn_W2, L0_ffn_b2,
           L0_c, L0_wmod):
    import concourse.bacc as bacc
    from concourse.bass_utils import run_bass_kernel_spmd

    a = lambda t: np.asarray(t)
    w = np.zeros((P, W_END), np.float32)
    wq, wk = a(L0_attn_Wq).T, a(L0_attn_Wk).T
    bq, bk = a(L0_attn_bq), a(L0_attn_bk)
    for n, (m, bias) in enumerate(((wq, bq), (wk, bk))):
        for half in range(2):
            cols, at = slice(64 * half, 64 * half + 64), (2 * n + half) * P
            w[:, at:at + 64] = m[:, cols]
            w[:, at + 64:at + P] = m[:, cols]
            w[0:64, W_BIAS + 2 * n + half] = bias[cols]
            w[64:, W_BIAS + 2 * n + half] = bias[cols]
    w[:, W_V:W_V + D] = a(L0_attn_Wv).T
    w[:, W_O:W_O + D] = a(L0_attn_Wo).T
    for head in range(64 // DH):
        w[head * DH:(head + 1) * DH, W_ORF + head * M:W_ORF + (head + 1) * M] = a(L0_attn_orf).T
    w[:, W_GATE:W_GATE + E] = a(L0_ffn_gate_W)
    w[:, W_B1:W_B1 + E * FC] = a(L0_ffn_b1).reshape(E * FC, P).T
    w[:, W_CT:W_CT + B] = a(L0_c).T
    rows = np.concatenate([a(L0_attn_bv), a(L0_attn_bo), a(L0_ffn_gate_b), a(L0_ffn_b2).reshape(-1)])
    rows = np.ascontiguousarray(np.broadcast_to(rows, (P, R_END)))

    ins = {"x": a(L0_attn_x), "weights": w, "consts": _constants(), "rows": rows, "wmod": a(L0_wmod),
           "w1": a(L0_ffn_W1), "w2": a(L0_ffn_W2)}
    nc = bacc.Bacc("TRN2", target_bir_lowering=False, num_devices=1)
    arrays = {f"in_{n}": np.ascontiguousarray(v) for n, v in ins.items()}
    aps = [nc.dram_tensor(n, v.shape, mybir.dt.from_np(v.dtype), kind="ExternalInput").ap()
           for n, v in arrays.items()]
    out = nc.dram_tensor("out", _OUT, F32, kind="ExternalOutput").ap()
    program(nc, aps, [out])
    r = run_bass_kernel_spmd(nc, [arrays], core_ids=[0])
    return r.results[0]["out"]
```

```python
from contextlib import ExitStack

import numpy as np

import concourse.bass as bass
from concourse import mybir

F32 = mybir.dt.float32
BF16 = mybir.dt.bfloat16
I32 = mybir.dt.int32
ACT = mybir.ActivationFunctionType
ALU = mybir.AluOpType
AX = mybir.AxisListType

B, L, D = 16, 512, 128
NH, DH, M = 16, 8, 32
E, DFF = 8, 512
P = 128
LT = L // P
NT = B * LT
NC = NH * M // P
CW = D // NC
FC = DFF // P
NBLK = NT + E
U = 8
R4 = 4
PITCH = NT * P + P
PADROW = E * PITCH
H2, X2, GT, ID, PW = 0, D, 2 * D, 3 * D, 3 * D + 8
NOROW = 1 << 20
FEPS = 1e-6
LNEPS = 1e-5
GMIN = 0.25
WB2, WB1 = DFF, DFF + D
WB = WB1 + FC
KP = P + 2
ROWS = 4
GA, SB, CB, GB = range(ROWS)

W_QA, W_QB, W_KA, W_KB, W_V, W_O = (i * P for i in range(6))
W_ORF = 6 * P
W_GATE = W_ORF + 2 * P
W_BIAS = W_GATE + CW
W_CT = W_BIAS + 4
W_END = W_CT + B
C_ID, C_MASK, C_TRI, C_NORM = 0, P, 2 * P, 3 * P
C_PREF = C_NORM + 2 * P
C_LIST = C_PREF + E
C_BLK = C_LIST + E
C_NUM = C_BLK + NBLK
C_PAD = C_NUM + LT
C_END = C_PAD + 1
R_BV, R_BO, R_GB = 0, D, 2 * D
R_END = R_GB + E


class Batch:

    def __init__(self, i, r):
        self.i, self.r = i, r
        self.v, self.half, self.par = 2 * i + r, i + r // 2, r % 2

    def __add__(self, n):
        return Batch(self.i, self.r + n)


def over_batches(eng, batch):
    batch(Batch(0, 0), first=True)
    batch(Batch(0, 1), second=True)
    batch(Batch(0, 2))
    with eng.Fori(1, B // 2 - 1) as i:
        batch(Batch(i, 1))
        batch(Batch(i, 2))
    batch(Batch(B // 2 - 1, 1), last=True)


class Steps:

    def __init__(self, eng, sem, base):
        self.eng, self.sem, self.base, self.n = eng, sem, base, 0

    def mark(self, instruction):
        instruction.then_inc(self.sem, 1)
        self.n += 1

    def wait(self):
        self.eng.wait_ge(self.sem, self.base + self.n)


def build(nc, x, weights, consts, rows, wmod, firsts, w2, out):
    lists = nc.dram_tensor("experts_lists", [PADROW + P, PW], F32).ap()
    mods = nc.dram_tensor("modulation_rows", [B, ROWS * D], F32).ap()

    with ExitStack() as ctx:
        def sb(name, shape, dt=F32):
            return ctx.enter_context(nc.sbuf_tensor(name, shape, dt))

        def pb(name):
            return ctx.enter_context(nc.psum_tensor(name, [P, 512], F32))

        def sem(name):
            return ctx.enter_context(nc.semaphore(name))

        xall = sb("xall", [P, NT, D])
        modb = sb("modb", [P, B, ROWS, D])
        wsb = sb("wsb", [P, W_END])
        csb = sb("csb", [P, C_END])
        rsb = sb("rsb", [P, R_END])
        firsts_sb = sb("firsts_sb", [P, E * WB])
        w2sb = sb("w2sb", [P, E * DFF])
        feat_w = sb("feat_w", [P, 2 * P])
        ones32 = sb("ones32", [P, CW])
        mhalf = sb("mhalf", [P, LT])
        padding = sb("padding", [P, PW])
        wmod_sb = sb("wmod_sb", [P, 6 * D])
        silu = sb("silu", [P, 3, B])
        modrow = sb("modrow", [B, ROWS, D])
        gsign = sb("gsign", [B, 2, D])
        ca1 = sb("ca1", [P, B])
        sa = sb("sa", [P, B])
        st1 = sb("st1", [P, LT, 6])
        mv1 = sb("mv1", [P, LT, 3])
        ve1 = sb("ve1", [P, LT])
        rstd1 = sb("rstd1", [P, LT])
        st2 = sb("st2", [P, LT, 6])
        mv2 = sb("mv2", [P, LT, 3])
        ve2 = sb("ve2", [P, LT])
        rstd2 = sb("rstd2", [P, LT])
        xn1 = sb("xn1", [P, LT, D])
        xn2 = sb("xn2", [P, LT, D])
        hT = sb("hT", [P, L])
        stack = [sb(f"stack{i}", [P, L]) for i in range(4)]
        v_sb = sb("v_sb", [P, LT, D])
        kf = sb("kf", [P, LT, NC, KP])
        qf = sb("qf", [P, NC, L])
        kvT = sb("kvT", [P, 2 * P])
        kvsum = sb("kvsum", [P, 2])
        kveps = sb("kveps", [P, 2])
        kvm = sb("kvm", [P, 2 * P])
        den = sb("den", [P, L])
        rden = sb("rden", [P, L])
        oT = sb("oT", [P, L])
        wo = sb("wo", [P, D])
        bog = sb("bog", [P, D])
        pay = [sb(f"pay{n}", [P, LT, PW]) for n in range(2)]
        h2T = sb("h2T", [P, L])
        lgT = sb("lgT", [P, P])
        tri = sb("tri", [P, P], BF16)
        ones_bf = sb("ones_bf", [P, P], BF16)
        lg = sb("lg", [P, LT, E])
        top = sb("top", [P, LT])
        eq = sb("eq", [P, LT, E])
        oh = sb("oh", [P, LT, E], BF16)
        seen = sb("seen", [P, E], BF16)
        ohsum = sb("ohsum", [P, E])
        rk = sb("rk", [P, LT, E])
        slot_f = sb("slot_f", [P, LT])
        slot = [sb(f"slot{n}", [P, LT], I32) for n in range(2)]
        num = sb("num", [P, LT])
        cnt_i = sb("cnt_i", [P, E], I32)
        cnt_b = sb("cnt_b", [P, E], I32)
        nblk = sb("nblk", [P, E])
        endblk = sb("endblk", [P, E])
        blk_ge = sb("blk_ge", [P, NBLK, E])
        blk_f = sb("blk_f", [P, NBLK])
        blk_r = sb("blk_r", [P, NBLK])
        blk_e = sb("blk_e", [P, NBLK], I32)
        blk_row = sb("blk_row", [P, NBLK], I32)
        xin = [sb(f"xin{u}", [P, PW]) for u in range(U)]
        xT = [sb(f"xT{u}", [P, P]) for u in range(2)]
        firsts_c = [sb(f"firsts_c{u}", [P, WB]) for u in range(R4)]
        g = [qf[:, u, :] for u in range(R4)]
        yb = [sb(f"yb{u}", [P, D]) for u in range(R4)]
        ids = [sb(f"ids{u}", [P, 1], I32) for u in range(R4)]

        F = [pb("ps_feat0"), pb("ps_feat1")]
        KV, G = pb("ps_kv"), pb("ps_den")
        H, I = pb("ps_out"), pb("ps_gate")
        PJ = [pb("ps_proj0"), pb("ps_proj1")]
        HID = [F[0], F[1], KV, G]
        XT = [H, I]
        Y = PJ

        ident = csb[:, C_ID:C_ID + P]
        mask = csb[:, C_MASK:C_MASK + P]

        s_w = sem("weights_in")
        s_c = sem("consts_in")
        s_r = sem("rows_in")
        s_wm = sem("wmod_in")
        s_w1 = sem("w1_in")
        s_w2 = sem("w2_in")
        s_x = [sem("x_in_even"), sem("x_in_odd")]
        s_mrow = sem("mod_rows_out")
        s_mb = sem("mod_rows_in")
        s_set = sem("setup_step")
        s_pset = sem("pool_setup")
        s_fw = sem("feature_weights")
        s_silue = sem("silu_exp")
        s_silu = sem("silu_ready")
        s_modp = sem("mod_products")
        s_modr = sem("mod_rows_ready")
        s_cols = sem("mod_columns_ready")
        s_pad = sem("padding_out")
        s_ln1 = sem("ln1_step")
        s_ln2 = sem("ln2_step")
        s_var1 = sem("var1_ready")
        s_var2 = sem("var2_ready")
        s_rstd1 = sem("rstd1_ready")
        s_rstd2 = sem("rstd2_ready")
        s_xn1 = sem("xn1_ready")
        s_xn2 = sem("xn2_ready")
        s_t1 = sem("xn1_transposed")
        s_hT = sem("hT_ready")
        s_proj = sem("projections")
        s_qv = sem("q_values")
        s_kval = sem("k_values")
        s_sq = sem("stack_squares")
        s_v = sem("v_ready")
        s_feat = sem("feature_products")
        s_exp = sem("features_ready")
        s_kv = sem("kv_product")
        s_kvs = sem("kv_step")
        s_kvT = sem("kvT_ready")
        s_kvt = sem("kv_transposed")
        s_kvm = sem("kvm_ready")
        s_eps = sem("kveps_ready")
        s_den = sem("den_product")
        s_num = sem("num_product")
        s_denp = sem("den_ready")
        s_rden = sem("rden_ready")
        s_oT = sem("oT_ready")
        s_wo = sem("wo_ready")
        s_bog = sem("bog_ready")
        s_xb = sem("xb_ready")
        s_op = sem("out_product")
        s_x2 = sem("x2_ready")
        s_h2m = sem("h2_scaled")
        s_h2 = sem("h2_ready")
        s_h2t = sem("h2_transposed")
        s_h2T = sem("h2T_ready")
        s_gb = sem("gate_rows_ready")
        s_lg = sem("gate_product")
        s_lgT = sem("gateT_ready")
        s_lgt = sem("gate_transposed")
        s_rt = sem("routing_step")
        s_oh = sem("onehot_ready")
        s_rank = sem("rank_products")
        s_seen = sem("seen_updated")
        s_slot = sem("slots_ready")
        s_scat = [sem("rows_scattered_even"), sem("rows_scattered_odd")]
        s_end = sem("table_step")
        s_cnt = sem("count_product")
        s_cnti = sem("counts_ready")
        s_blk = sem("block_table_ready")
        s_xin = [sem(f"block_in{u}") for u in range(U)]
        s_bt = sem("block_transposed")
        s_bT = sem("block_T_ready")
        s_fc = sem("firsts_copied")
        s_hid = sem("hidden_product")
        s_gelu = sem("hidden_ready")
        s_y = sem("result_product")
        s_yb = sem("result_ready")
        s_yst = sem("result_step")
        s_yout = [sem(f"result_out{u}") for u in range(R4)]

        block = ctx.enter_context(nc.Block())

        def apart(eng):
            eng.wait_ge(s_w, 16)

        def snapped(eng, value):
            return value if isinstance(value, int) else eng.snap(value)

        @block.sync
        def _(sp):
            sp.dma_start(wsb[:], weights).then_inc(s_w, 16)
            sp.dma_start(wmod_sb[:], wmod).then_inc(s_wm, 16)
            sp.dma_start(csb[:], consts).then_inc(s_c, 16)
            xv = x.rearrange("b (p t) d -> b p t d", t=LT)

            def load_x(b, parity):
                sp.dma_start(xall[:, bass.ds(b * LT, LT), :], xv[bass.ds(b, 1), :, :, :])\
                    .then_inc(s_x[parity], 16)

            load_x(0, 0)
            load_x(1, 1)
            sp.dma_start(rsb[:], rows).then_inc(s_r, 16)
            sp.wait_ge(s_modr, 1)
            sp.dma_start(mods, modrow[:, :, :].rearrange("b r d -> b (r d)")).then_inc(s_mrow, 16)
            sp.wait_ge(s_mrow, 16)
            sp.dma_start(modb[:, :, :, :].rearrange("p b r d -> p (b r d)"),
                         mods.rearrange("b n -> (b n)").unsqueeze(0).to_broadcast([P, B * ROWS * D]))\
                .then_inc(s_mb, 16)
            with sp.Fori(1, B // 2) as i:
                for parity in range(2):
                    sp.wait_ge(s_x[parity], 16 * i)
                    load_x(2 * i + parity, parity)
            sp.dma_start(firsts_sb[:], firsts).then_inc(s_w1, 16)
            sp.dma_start(w2sb[:, :].rearrange("p (e c d) -> p e c d", e=E, c=FC),
                         w2.rearrange("e (c p) d -> p e c d", p=P)).then_inc(s_w2, 16)
            sp.wait_ge(s_pset, 5)
            sp.dma_start(lists[PADROW:PADROW + P, :], padding[:]).then_inc(s_pad, 16)

            sp.wait_ge(s_cnti, 1)
            for e in range(E):
                count = sp.value_load(cnt_i[0:1, e:e + 1], min_val=0, max_val=NT * P)
                sp.dma_start(lists[bass.ds(count + e * PITCH, P), :], padding[:]).then_inc(s_pad, 16)

            def load_block(k, u):
                row = sp.value_load(blk_row[0:1, bass.ds(k, 1)], min_val=0, max_val=PADROW)
                sp.dma_start(xin[u][:], lists[bass.ds(row, P), :]).then_inc(s_xin[u], 16)

            for n in range(2):
                sp.wait_ge(s_scat[n], 16 * LT * B // 2)
            sp.wait_ge(s_pad, 16 * (E + 1))
            sp.wait_ge(s_blk, 1)
            for u in range(U):
                load_block(u, u)
            with sp.Fori(0, NBLK // U - 1) as i:
                for u in range(U):
                    sp.wait_ge(s_yb, i * U + (u + 1))
                    load_block(i * U + (U + u), u)

        @block.gpsimd
        def _(pool):
            g_ = nc.gpsimd
            g_.memset(mhalf[:], -0.5).then_inc(s_pset, 1)
            g_.memset(padding[:], 0.0).then_inc(s_pset, 1)
            for n in range(2):
                g_.memset(pay[n][:, :, ID:PW], 0.0).then_inc(s_pset, 1)

            def rstd(b, which):
                ve, out_, ready, done = ((ve1, rstd1, s_var1, s_rstd1), (ve2, rstd2, s_var2, s_rstd2))[which]
                pool.wait_ge(ready, b.v + 1)
                g_.tensor_tensor(out_[:], ve[:], mhalf[:], ALU.pow).then_inc(done, 1)

            def gated(b, first=False):
                ga = modb[:, bass.ds(b.v, 1), GA, :]
                if not first:
                    apart(pool)
                    pool.wait_ge(s_xb, b.v)
                g_.tensor_tensor(bog[:], rsb[:, R_BO:R_BO + D], ga.squeeze(1), ALU.mult).then_inc(s_bog, 1)
                apart(pool)
                pool.wait_ge(s_bog, b.v + 1)
                pool.wait_ge(s_xn1, b.v + 1)
                xt = xall[:, bass.ds(b.v * LT, LT), :]
                g_.tensor_tensor(xt, xt, bog[:, :].unsqueeze(1).to_broadcast([P, LT, D]), ALU.add)\
                    .then_inc(s_xb, 1)
                if not first:
                    apart(pool)
                    pool.wait_ge(s_op, b.v)
                g_.tensor_tensor(wo[:], wsb[:, W_O:W_O + D], ga.squeeze(1), ALU.mult).then_inc(s_wo, 1)

            def experts_input(b):
                h2 = pay[b.par][:, :, H2:H2 + D]
                apart(pool)
                pool.wait_ge(s_xn2, b.v + 1)
                g_.tensor_tensor(h2, xn2[:], modb[:, bass.ds(b.v, 1), CB, :].to_broadcast([P, LT, D]), ALU.mult)\
                    .then_inc(s_h2m, 1)
                apart(pool)
                pool.wait_ge(s_h2m, b.v + 1)
                g_.tensor_tensor(h2, h2, modb[:, bass.ds(b.v, 1), SB, :].to_broadcast([P, LT, D]), ALU.add)\
                    .then_inc(s_h2, 1)

            def scatter(b):
                value = snapped(pool, b.v + 1)
                apart(pool)
                pool.wait_ge(s_slot, value)
                pool.wait_ge(s_gb, value)
                for t in range(LT):
                    g_.indirect_dma_start(out=lists, in_=pay[b.par][:, t, :], in_offset=None,
                                          out_offset=bass.IndirectOffsetOnAxis(ap=slot[b.par][:, t:t + 1], axis=0))\
                        .then_inc(s_scat[b.par], 16)

            def batch(b, first=False, second=False, last=False):
                if not last:
                    rstd(b + 1, 0)
                if first:
                    pool.wait_ge(s_r, 16)
                    pool.wait_ge(s_mb, 16)
                gated(b, first)
                if not first:
                    rstd(b + -1, 1)
                    experts_input(b + -1)
                if not first and not second:
                    scatter(b + -2)

            rstd(Batch(0, 0), 0)
            over_batches(pool, batch)
            end = Batch(0, B)
            rstd(end + -1, 1)
            experts_input(end + -1)
            scatter(end + -2)
            scatter(end + -1)

            rows_out = out.rearrange("b l d -> (b l) d")
            last_row = pool.to_reg(B * L - 1)

            def store(k, u):
                value = pool.to_reg(2 * k + 2)
                apart(pool)
                pool.wait_ge(s_yst, value)
                y = yb[u % R4]
                g_.tensor_tensor(y[:], y[:], xin[u][:, X2:X2 + D], ALU.add).then_inc(s_yb, 1)
                value = pool.to_reg(k + 1)
                apart(pool)
                pool.wait_ge(s_yb, value)
                g_.indirect_dma_start(out=rows_out, in_=yb[u % R4][:], in_offset=None,
                                      out_offset=bass.IndirectOffsetOnAxis(ap=ids[u % R4][:, 0:1], axis=0),
                                      bounds_check=last_row, oob_is_err=False).then_inc(s_yout[u % R4], 16)

            with pool.Fori(0, NBLK // U) as i:
                for u in range(U):
                    store(i * U + u, u)
            for u in range(R4):
                pool.wait_ge(s_yout[u], 16 * NBLK // R4)

        @block.scalar
        def _(act):
            a = nc.scalar
            act.wait_ge(s_w, 16)
            a.activation(silu[:, 0, :], wsb[:, W_CT:W_CT + B], ACT.Exp, scale=-1.0).then_inc(s_silue, 1)

            def squares(b, i):
                act.wait_ge(s_proj, 5 * b.v + i + 1)
                a.activation(stack[i][64:128, :], PJ[i % 2][64:128, :], ACT.Square,
                             bias=wsb[64:128, W_BIAS + i:W_BIAS + i + 1]).then_inc(s_sq, 1)

            def values(b, i):
                a.activation(stack[i][0:64, :], PJ[i % 2][0:64, :], ACT.Identity,
                             bias=wsb[0:64, W_BIAS + i:W_BIAS + i + 1]).then_inc(s_kval, 1)

            def feature(b, j):
                act.wait_ge(s_feat, 2 * NC * b.v + j + 1)
                src = F[j % 2][:, :]
                if j < LT:
                    dst, src = kf[:, j, :, 0:P], src.rearrange("p (c m) -> p c m", c=NC)
                else:
                    dst = qf[:, j - LT, :]
                a.activation(dst, src, ACT.Exp).then_inc(s_exp, 1)

            def h2T_copy(b):
                act.wait_ge(s_h2t, b.v + 1)
                a.activation(h2T[:], I[:], ACT.Copy).then_inc(s_h2T, 1)

            def gate_rows(b):
                if not (isinstance(b.half, int) and b.half == 0):
                    value = snapped(act, 16 * LT * b.half)
                    apart(act)
                    act.wait_ge(s_scat[b.par], value)
                a.activation(pay[b.par][:, :, GT:GT + D],
                             modb[:, bass.ds(b.v, 1), GB, :].to_broadcast([P, LT, D]), ACT.Copy).then_inc(s_gb, 1)

            def batch(b, first=False, second=False, last=False):
                for j in range(2 * NC):
                    feature(b, j)
                if not last:
                    squares(b + 1, 0)
                act.wait_ge(s_kvt, b.v + 1)
                a.activation(kvm[:], G[:, 0:2 * P], ACT.Copy).then_inc(s_kvm, 1)
                if not last:
                    squares(b + 1, 1)
                if not first:
                    h2T_copy(b + -1)
                act.wait_ge(s_den, b.v + 1)
                act.wait_ge(s_eps, b.v + 1)
                a.activation(den[:], G[:], ACT.Identity, bias=kveps[:, 1:2]).then_inc(s_denp, 1)
                if not last:
                    for n in (2, 3):
                        squares(b + 1, n)
                        values(b + 1, n)
                if first:
                    act.wait_ge(s_mb, 16)
                if not first:
                    gate_rows(b + -1)

            for n in range(4):
                squares(Batch(0, 0), n)
                if n >= 2:
                    values(Batch(0, 0), n)
            over_batches(act, batch)
            end = Batch(0, B)
            h2T_copy(end + -1)
            gate_rows(end + -1)

            def copy_xT(k, u):
                act.wait_ge(s_bt, k + 1)
                a.activation(xT[u % 2][:], XT[u % 2][:, 0:P], ACT.Copy).then_inc(s_bT, 1)

            def turn(i, last=False):
                for u in range(U):
                    if not (last and u == U - 1):
                        copy_xT(i * U + (u + 1), u + 1)
                    act.wait_ge(s_hid, i * U + (u + 1))
                    for c in range(FC):
                        ins = a.activation(g[u % R4][:, c * P:(c + 1) * P], HID[u % R4][:, c * P:(c + 1) * P],
                                           ACT.Gelu, bias=firsts_c[u % R4][:, WB1 + c:WB1 + c + 1])
                    ins.then_inc(s_gelu, 1)

            act.wait_ge(s_blk, 1)
            copy_xT(0, 0)
            with act.Fori(0, NBLK // U - 1) as i:
                turn(i)
            turn(NBLK // U - 1, last=True)

        @block.vector
        def _(dve):
            v = nc.vector

            v.memset(ones32[:], 1.0).then_inc(s_set, 1)
            v.memset(kf[:, :, :, P:KP], FEPS).then_inc(s_set, 1)
            v.memset(ones_bf[:], 1.0).then_inc(s_set, 1)
            v.memset(seen[:], 0.0).then_inc(s_set, 1)
            dve.wait_ge(s_silue, 1)
            v.tensor_scalar(silu[:, 1, :], silu[:, 0, :], 1.0, None, ALU.add).then_inc(s_set, 1)
            dve.wait_ge(s_set, 5)
            v.reciprocal(silu[:, 2, :], silu[:, 1, :]).then_inc(s_set, 1)
            dve.wait_ge(s_set, 6)
            v.tensor_tensor(silu[:, 0, :], silu[:, 2, :], wsb[:, W_CT:W_CT + B], ALU.mult).then_inc(s_silu, 1)
            dve.wait_ge(s_c, 16)
            v.tensor_copy(num[:], csb[:, C_NUM:C_NUM + LT]).then_inc(s_fw, 1)
            dve.wait_ge(s_pset, 4)
            v.tensor_copy(padding[:, ID:ID + 1].bitcast(I32), csb[:, C_PAD:C_PAD + 1]).then_inc(s_pset, 1)
            v.scalar_tensor_tensor(out=feat_w[:], in0=wsb[:, W_ORF:W_ORF + 2 * P], scalar=float(DH ** -0.25),
                                   in1=csb[:, C_NORM:C_NORM + 2 * P], op0=ALU.mult, op1=ALU.add).then_inc(s_fw, 1)
            v.tensor_copy(tri[:], csb[:, C_TRI:C_TRI + P]).then_inc(s_fw, 1)
            dve.wait_ge(s_modp, 1)
            v.tensor_copy(sa[:], F[0][:, 0:B])
            v.tensor_scalar(ca1[:], F[0][:, B:2 * B], 1.0, None, ALU.add).then_inc(s_cols, 1)
            v.tensor_copy(modrow[:, SB, :], I[0:B, 0:D])
            v.tensor_scalar(modrow[:, CB, :], I[0:B, D:2 * D], 1.0, None, ALU.add)
            gates = [(n, row, src[0:B, 2 * D:3 * D]) for n, (row, src) in enumerate(((GA, H), (GB, I)))]
            for n, row, gate in gates:
                ins = v.tensor_scalar(gsign[:, n, :], gate, 0.0, 2.0, ALU.is_ge, ALU.mult)
            ins.then_inc(s_set, 1)
            dve.wait_ge(s_set, 7)
            v.tensor_scalar(gsign[:, :, :], gsign[:, :, :], -1.0, None, ALU.add).then_inc(s_set, 1)
            dve.wait_ge(s_set, 8)
            for n, row, gate in gates:
                ins = v.tensor_tensor(modrow[:, row, :], gate, gsign[:, n, :], ALU.mult)
            ins.then_inc(s_set, 1)
            dve.wait_ge(s_set, 9)
            for n, row, gate in gates:
                ins = v.scalar_tensor_tensor(out=modrow[:, row, :], in0=modrow[:, row, :], scalar=GMIN,
                                             in1=gsign[:, n, :], op0=ALU.max, op1=ALU.mult)
            ins.then_inc(s_modr, 1)

            def stats(b, which):
                st, mv, ve, step, ready = ((st1, mv1, ve1, s_ln1, s_var1), (st2, mv2, ve2, s_ln2, s_var2))[which]
                s = Steps(dve, step, 3 * b.v)
                for t in range(LT):
                    ins = v.bn_stats(st[:, t, :], ln_row(b, which, t))
                s.mark(ins)
                s.wait()
                v.tensor_tensor(mv[:, :, 0:2], st[:, :, 1:3], st[:, :, 4:6], ALU.add)
                s.mark(v.tensor_tensor(mv[:, :, 2], st[:, :, 1], st[:, :, 4], ALU.subtract))
                s.wait()
                v.tensor_scalar(mv[:, :, 0], mv[:, :, 0], 0.5, None, ALU.mult)
                v.tensor_scalar(mv[:, :, 1], mv[:, :, 1], 1.0 / D, LNEPS, ALU.mult, ALU.add)
                s.mark(v.tensor_tensor(mv[:, :, 2], mv[:, :, 2], mv[:, :, 2], ALU.mult))
                s.wait()
                v.scalar_tensor_tensor(out=ve[:], in0=mv[:, :, 2], scalar=0.25, in1=mv[:, :, 1],
                                       op0=ALU.mult, op1=ALU.add).then_inc(ready, 1)

            def ln_row(b, which, t):
                if which:
                    return pay[b.par][:, t, X2:X2 + D]
                return xall[:, bass.ds(b.v * LT + t, 1), :].squeeze(1)

            def first_stats(b):
                value = snapped(dve, 16 * (b.half + 1))
                apart(dve)
                dve.wait_ge(s_x[b.par], value)
                stats(b, 0)

            def normalise(b, which, first=False):
                mv, rstd, xn, rdy, done = ((mv1, rstd1, xn1, s_rstd1, s_xn1), (mv2, rstd2, xn2, s_rstd2, s_xn2))[which]
                dve.wait_ge(rdy, b.v + 1)
                if not first:
                    dve.wait_ge(s_h2m if which else s_t1, b.v)
                for t in range(LT):
                    ins = v.tensor_scalar(xn[:, t, :], ln_row(b, which, t), mv[:, t, 0:1], rstd[:, t:t + 1],
                                          ALU.subtract, ALU.mult)
                ins.then_inc(done, 1)

            def modulate(b):
                dve.wait_ge(s_t1, b.v + 1)
                v.tensor_scalar(hT[:], H[:], ca1[:, bass.ds(b.v, 1)], sa[:, bass.ds(b.v, 1)], ALU.mult, ALU.add)\
                    .then_inc(s_hT, 1)

            def values(b, i):
                dve.wait_ge(s_proj, 5 * b.v + i + 1)
                v.tensor_scalar(stack[i][0:64, :], PJ[i % 2][0:64, :], wsb[0:64, W_BIAS + i:W_BIAS + i + 1], None,
                                ALU.add).then_inc(s_qv, 1)

            def v_values(b):
                dve.wait_ge(s_proj, 5 * b.v + 5)
                v.tensor_tensor(v_sb[:], PJ[0][:, :].rearrange("p (t d) -> p t d", t=LT),
                                rsb[:, R_BV:R_BV + D].unsqueeze(1).to_broadcast([P, LT, D]), ALU.add).then_inc(s_v, 1)

            def kv_values(b, first=False):
                dve.wait_ge(s_kv, b.v + 1)
                if not first:
                    dve.wait_ge(s_denp, b.v)
                v.scalar_tensor_tensor(out=kvT[:, 0:P], in0=KV[:, 0:P], scalar=KV[:, P:P + 1], in1=mask,
                                       op0=ALU.add, op1=ALU.mult, accum_out=kvsum[:, 0:1])
                v.scalar_tensor_tensor(out=kvT[:, P:2 * P], in0=KV[:, 256:256 + P], scalar=float(L * FEPS), in1=mask,
                                       op0=ALU.add, op1=ALU.mult, accum_out=kvsum[:, 1:2]).then_inc(s_kvT, 1)
                dve.wait_ge(s_kvT, b.v + 1)
                v.tensor_scalar(kveps[:], kvsum[:], FEPS, None, ALU.mult).then_inc(s_eps, 1)

            def attention(b):
                dve.wait_ge(s_denp, b.v + 1)
                v.reciprocal(rden[:], den[:]).then_inc(s_rden, 1)
                dve.wait_ge(s_rden, b.v + 1)
                dve.wait_ge(s_num, b.v + 1)
                v.scalar_tensor_tensor(out=oT[:], in0=KV[:], scalar=kveps[:, 0:1], in1=rden[:],
                                       op0=ALU.add, op1=ALU.mult).then_inc(s_oT, 1)

            def residual(b):
                dve.wait_ge(s_op, b.v + 1)
                dve.wait_ge(s_xb, b.v + 1)
                if not (isinstance(b.half, int) and b.half == 0):
                    dve.wait_ge(s_scat[b.par], 16 * LT * b.half)
                v.tensor_tensor(pay[b.par][:, :, X2:X2 + D], H[:, :].rearrange("p (t d) -> p t d", t=LT),
                                xall[:, bass.ds(b.v * LT, LT), :], ALU.add).then_inc(s_x2, 1)

            def second_stats(b):
                value = snapped(dve, b.v + 1)
                apart(dve)
                dve.wait_ge(s_x2, value)
                stats(b, 1)

            def gateT(b):
                dve.wait_ge(s_lg, b.v + 1)
                v.tensor_copy(lgT[:], I[:, 0:P]).then_inc(s_lgT, 1)

            def experts(b):
                s = Steps(dve, s_rt, 8 * b.v)
                tb = lambda r: r.unsqueeze(1).to_broadcast([P, LT, E])
                eb = lambda r: r.unsqueeze(2).to_broadcast([P, LT, E])
                dve.wait_ge(s_lgt, b.v + 1)
                s.mark(v.tensor_tensor(lg[:], I[:, P:2 * P].rearrange("p (t c) -> p t c", t=LT)[:, :, 0:E],
                                       tb(rsb[:, R_GB:R_GB + E]), ALU.add))
                s.wait()
                s.mark(v.tensor_reduce(out=top[:], in_=lg[:], op=ALU.max, axis=AX.X))
                s.wait()
                s.mark(v.tensor_tensor(eq[:], lg[:], eb(top[:, :]), ALU.is_ge))
                s.wait()
                s.mark(v.tensor_tensor(eq[:], eq[:], tb(csb[:, C_PREF:C_PREF + E]), ALU.mult))
                s.wait()
                s.mark(v.tensor_reduce(out=top[:], in_=eq[:], op=ALU.max, axis=AX.X))
                s.wait()
                v.tensor_tensor(oh[:], eq[:], eb(top[:, :]), ALU.is_equal).then_inc(s_oh, 1)

            def slots(b):
                s = Steps(dve, s_rt, 8 * b.v + 5)
                dve.wait_ge(s_rank, b.v + 1)
                v.tensor_reduce(out=ohsum[:], in_=oh[:, :, :].rearrange("p t e -> p e t"), op=ALU.add, axis=AX.X)
                s.mark(v.tensor_tensor(rk[:], I[:, 2 * P:2 * P + LT * E].rearrange("p (t e) -> p t e", t=LT),
                                       csb[:, C_LIST:C_LIST + E].unsqueeze(1).to_broadcast([P, LT, E]), ALU.add))
                s.wait()
                v.tensor_tensor(seen[:], seen[:], ohsum[:], ALU.add).then_inc(s_seen, 1)
                v.tensor_copy(pay[b.par][:, :, ID:ID + 1].bitcast(I32), num[:, :].unsqueeze(2))
                s.mark(v.tensor_tensor(rk[:], rk[:], oh[:], ALU.mult))
                s.wait()
                v.tensor_scalar(num[:], num[:], float(L), None, ALU.add)
                s.mark(v.tensor_reduce(out=slot_f[:], in_=rk[:], op=ALU.add, axis=AX.X))
                s.wait()
                v.tensor_copy(slot[b.par][:], slot_f[:]).then_inc(s_slot, 1)

            def batch(b, first=False, second=False, last=False):
                if not last:
                    first_stats(b + 1)
                if not first and not second:
                    experts(b + -2)
                if not first:
                    residual(b + -1)
                if not last:
                    normalise(b + 1, 0)
                if not first:
                    second_stats(b + -1)
                if not last:
                    modulate(b + 1)
                if not first:
                    normalise(b + -1, 1, first=second)
                kv_values(b, first)
                if not first and not second:
                    slots(b + -2)
                if not last:
                    values(b + 1, 0)
                    values(b + 1, 1)
                attention(b)
                if not last:
                    v_values(b + 1)
                if not first:
                    gateT(b + -1)

            start, end = Batch(0, 0), Batch(0, B)
            first_stats(start)
            normalise(start, 0, first=True)
            dve.wait_ge(s_cols, 1)
            modulate(start)
            values(start, 0)
            values(start, 1)
            dve.wait_ge(s_r, 16)
            v_values(start)
            over_batches(dve, batch)
            experts(end + -2)
            residual(end + -1)
            second_stats(end + -1)
            normalise(end + -1, 1)
            slots(end + -2)
            gateT(end + -1)
            experts(end + -1)
            slots(end + -1)

            s = Steps(dve, s_end, 0)
            dve.wait_ge(s_cnt, 1)
            v.tensor_copy(cnt_i[:], F[0][:, 0:E]).then_inc(s_cnti, 1)
            s.mark(v.tensor_scalar(nblk[:], F[0][:, 0:E], float(P - 1), None, ALU.add))
            s.wait()
            s.mark(v.tensor_copy(cnt_b[:], nblk[:]))
            s.wait()
            s.mark(v.tensor_scalar(cnt_b[:], cnt_b[:], P.bit_length() - 1, None, ALU.arith_shift_right))
            s.wait()
            s.mark(v.tensor_copy(nblk[:], cnt_b[:]))
            s.wait()
            s.mark(v.tensor_tensor_scan(out=endblk[:], data0=ones32[:, 0:E], data1=nblk[:], initial=0.0,
                                        op0=ALU.mult, op1=ALU.add))
            s.wait()
            numbers = csb[:, C_BLK:C_BLK + NBLK]
            s.mark(v.tensor_tensor(blk_ge[:], numbers.unsqueeze(2).to_broadcast([P, NBLK, E]),
                                   endblk[:, :].unsqueeze(1).to_broadcast([P, NBLK, E]), ALU.is_ge))
            s.wait()
            s.mark(v.tensor_reduce(out=blk_f[:], in_=blk_ge[:], op=ALU.add, axis=AX.X))
            s.wait()
            s.mark(v.tensor_tensor(blk_ge[:], blk_ge[:], nblk[:, :].unsqueeze(1).to_broadcast([P, NBLK, E]), ALU.mult))
            s.wait()
            s.mark(v.tensor_reduce(out=blk_r[:], in_=blk_ge[:], op=ALU.add, axis=AX.X))
            s.wait()
            s.mark(v.scalar_tensor_tensor(out=blk_r[:], in0=blk_r[:], scalar=-1.0, in1=numbers,
                                          op0=ALU.mult, op1=ALU.add))
            s.wait()
            s.mark(v.scalar_tensor_tensor(out=blk_r[:], in0=blk_f[:], scalar=float(PITCH // P), in1=blk_r[:],
                                          op0=ALU.mult, op1=ALU.add))
            s.wait()
            v.tensor_scalar(blk_f[:], blk_f[:], float(E - 1), None, ALU.min)
            s.mark(v.tensor_scalar(blk_r[:], blk_r[:], float(P), float(PADROW), ALU.mult, ALU.min))
            s.wait()
            v.tensor_copy(blk_e[:], blk_f[:])
            v.tensor_copy(blk_row[:], blk_r[:]).then_inc(s_blk, 1)
            dve.wait_ge(s_blk, 1)
            dve.wait_ge(s_w1, 16)

            def expert_of(k):
                return dve.value_load(blk_e[0:1, bass.ds(k, 1)], min_val=0, max_val=E - 1)

            def copy_firsts(i, u):
                k = i * U + u
                e = expert_of(k)
                if not (isinstance(k, int) and k < R4):
                    apart(dve)
                    dve.wait_ge(s_yst, 2 * k - (2 * R4 - 1))
                v.tensor_copy(firsts_c[u % R4][:], firsts_sb[:, bass.ds(e * WB, WB)]).then_inc(s_fc, 1)

            def gated_result(i, u):
                k = i * U + u
                y, ring = yb[u % R4], u % R4
                dve.wait_ge(s_y, k + 1)
                if not (isinstance(k, int) and k < R4):
                    dve.wait_ge(s_yout[ring], 16 * (i * (U // R4) + u // R4))
                v.tensor_tensor(y[:], Y[u % 2][:, 0:D], firsts_c[ring][:, WB2:WB2 + D], ALU.add).then_inc(s_yst, 1)
                v.tensor_copy(ids[ring][:], xin[u % U][:, ID:ID + 1].bitcast(I32))
                dve.wait_ge(s_yst, 2 * k + 1)
                v.tensor_tensor(y[:], y[:], xin[u % U][:, GT:GT + D], ALU.mult).then_inc(s_yst, 1)

            def turn(i, first=False, last=False):
                for u in range(U):
                    if not (first and u < 2):
                        gated_result(i, u - 2)
                    if not (last and u >= U - 2):
                        copy_firsts(i, u + 2)

            copy_firsts(0, 0)
            copy_firsts(0, 1)
            turn(0, first=True)
            with dve.Fori(1, NBLK // U - 1) as i:
                turn(i)
            turn(NBLK // U - 1, last=True)
            for u in range(2):
                gated_result(NBLK // U - 1, U - 2 + u)

        @block.tensor
        def _(pe):
            mm, tr = nc.tensor.matmul, nc.tensor.transpose

            pe.wait_ge(s_silu, 1)
            pe.wait_ge(s_wm, 16)
            sc = silu[:, 0, :]
            mm(H[0:B, 0:3 * D], sc, wmod_sb[:, 0:3 * D], start=True, stop=True)
            mm(I[0:B, 0:3 * D], sc, wmod_sb[:, 3 * D:6 * D], start=True, stop=True)
            mm(F[0][:, 0:B], wmod_sb[:, 0:D], sc, start=True, stop=True)
            mm(F[0][:, B:2 * B], wmod_sb[:, D:2 * D], sc, start=True, stop=True).then_inc(s_modp, 1)

            def transpose_xn(b, first=False):
                pe.wait_ge(s_xn1, b.v + 1)
                if not first:
                    pe.wait_ge(s_x2, b.v - 1)
                for t in range(LT):
                    ins = tr(H[:, t * P:(t + 1) * P], xn1[:, t, :], ident)
                ins.then_inc(s_t1, 1)

            def project(b, i, first=False):
                if i == 0:
                    pe.wait_ge(s_hT, b.v + 1)
                    if not first:
                        pe.wait_ge(s_v, b.v)
                elif i == 1 and not first:
                    pe.wait_ge(s_kval, 2 * b.v)
                elif i in (2, 3):
                    pe.wait_ge(s_qv, 2 * b.v + i - 1)
                    pe.wait_ge(s_sq, 4 * b.v + i - 1)
                elif i == 4:
                    pe.wait_ge(s_kval, 2 * b.v + 1)
                if i < 4:
                    mm(PJ[i % 2][:, :], wsb[:, i * P:(i + 1) * P], hT[:], start=True, stop=True).then_inc(s_proj, 1)
                else:
                    for t in range(LT):
                        ins = mm(PJ[0][:, t * P:(t + 1) * P], hT[:, t * P:(t + 1) * P], wsb[:, W_V:W_V + D],
                                 start=True, stop=True)
                    ins.then_inc(s_proj, 1)

            def feature(b, j, first=False):
                if not (first and j < 2):
                    pe.wait_ge(s_exp, 2 * NC * b.v + j - 1)
                if j == 0:
                    pe.wait_ge(s_kval, 2 * b.v + 2)
                if j == LT:
                    pe.wait_ge(s_qv, 2 * b.v + 2)
                ps = F[j % 2]
                if j < LT:
                    for half in range(2):
                        ins = mm(ps[:, half * 2 * P:(half + 1) * 2 * P], stack[2 + half][:, j * P:(j + 1) * P],
                                 feat_w[:], start=True, stop=True)
                else:
                    c = j - LT
                    ins = mm(ps[:, :], feat_w[:, (c % 2) * P:(c % 2 + 1) * P], stack[c // 2][:], start=True, stop=True)
                ins.then_inc(s_feat, 1)

            def kv_product(b, first=False):
                pe.wait_ge(s_exp, 2 * NC * b.v + LT)
                pe.wait_ge(s_v, b.v + 1)
                if not first:
                    pe.wait_ge(s_oT, b.v)
                for t in range(LT):
                    for c in range(NC):
                        mm(KV[c * CW:(c + 1) * CW, 0:P + 1], v_sb[:, t, c * CW:(c + 1) * CW], kf[:, t, c, 0:P + 1],
                           start=(t == 0), stop=(t == LT - 1))
                for t in range(LT):
                    for c in range(NC):
                        ins = mm(KV[c * CW:(c + 1) * CW, 256:256 + P], ones32[:], kf[:, t, c, 0:P],
                                 start=(t == 0), stop=(t == LT - 1))
                ins.then_inc(s_kv, 1)

            def kv_transpose(b):
                pe.wait_ge(s_kvT, b.v + 1)
                for n in range(2):
                    ins = tr(G[:, n * P:(n + 1) * P], kvT[:, n * P:(n + 1) * P], ident)
                ins.then_inc(s_kvt, 1)

            def attend(b):
                pe.wait_ge(s_kvm, b.v + 1)
                pe.wait_ge(s_exp, 2 * NC * (b.v + 1))
                for c in range(NC):
                    ins = mm(G[c * CW:(c + 1) * CW, :], kvm[:, P + c * CW:P + (c + 1) * CW], qf[:, c, :],
                             start=True, stop=True)
                ins.then_inc(s_den, 1)
                for c in range(NC):
                    ins = mm(KV[c * CW:(c + 1) * CW, :], kvm[:, c * CW:(c + 1) * CW], qf[:, c, :],
                             start=True, stop=True)
                ins.then_inc(s_num, 1)

            def out_project(b, last=False):
                pe.wait_ge(s_oT, b.v + 1)
                pe.wait_ge(s_wo, b.v + 1)
                if not last:
                    pe.wait_ge(s_hT, b.v + 2)
                for t in range(LT):
                    ins = mm(H[:, t * P:(t + 1) * P], oT[:, t * P:(t + 1) * P], wo[:], start=True, stop=True)
                ins.then_inc(s_op, 1)

            def transpose_h2(b, first=False):
                pe.wait_ge(s_h2, b.v + 1)
                if not first:
                    pe.wait_ge(s_slot, b.v)
                for t in range(LT):
                    ins = tr(I[:, t * P:(t + 1) * P], pay[b.par][:, t, H2:H2 + D], ident)
                ins.then_inc(s_h2t, 1)

            def gate(b):
                pe.wait_ge(s_h2T, b.v + 1)
                for t in range(LT):
                    ins = mm(I[t * CW:(t + 1) * CW, 0:P], wsb[:, W_GATE:W_GATE + CW], h2T[:, t * P:(t + 1) * P],
                             start=True, stop=True)
                ins.then_inc(s_lg, 1)

            def gate_transpose(b):
                pe.wait_ge(s_lgT, b.v + 1)
                tr(I[:, P:2 * P], lgT[:], ident).then_inc(s_lgt, 1)

            def rank(b, first=False):
                pe.wait_ge(s_oh, b.v + 1)
                if not first:
                    pe.wait_ge(s_seen, b.v)
                out_ = I[:, 2 * P:2 * P + LT * E].rearrange("p (t e) -> p t e", t=LT)
                mm(out_, tri[:], oh[:], start=True, stop=False)
                for t in range(1, LT):
                    mm(out_[:, t:LT, :], ones_bf[:], oh[:, 0:LT - t, :], start=False, stop=False)
                mm(out_, ones_bf[:], seen[:, :].unsqueeze(1).to_broadcast([P, LT, E]), start=False, stop=True)\
                    .then_inc(s_rank, 1)

            def batch(b, first=False, second=False, last=False):
                feature(b, 0, first)
                feature(b, 1, first)
                if not first and not second:
                    gate_transpose(b + -2)
                if not first:
                    out_project(b + -1)
                for j in range(2, LT + 2):
                    feature(b, j)
                if not last:
                    transpose_xn(b + 1, first)
                kv_product(b, first)
                if not first and not second:
                    rank(b + -2, first=isinstance(b.v, int) and b.v == 2)
                feature(b, LT + 2)
                feature(b, LT + 3)
                if not last:
                    project(b + 1, 0)
                kv_transpose(b)
                if not last:
                    project(b + 1, 1)
                if not first:
                    transpose_h2(b + -1, first=second)
                attend(b)
                if not last:
                    project(b + 1, 2)
                    project(b + 1, 3)
                    project(b + 1, 4)
                if not first:
                    gate(b + -1)

            pe.wait_ge(s_modr, 1)
            pe.wait_ge(s_fw, 3)
            pe.wait_ge(s_set, 4)
            start, end = Batch(0, 0), Batch(0, B)
            transpose_xn(start, first=True)
            for i in range(5):
                project(start, i, first=True)
            over_batches(pe, batch)
            gate_transpose(end + -2)
            out_project(end + -1, last=True)
            rank(end + -2)
            transpose_h2(end + -1)
            gate(end + -1)
            gate_transpose(end + -1)
            rank(end + -1)

            pe.wait_ge(s_seen, B)
            mm(F[0][:, 0:E], ones_bf[:], seen[:], start=True, stop=True).then_inc(s_cnt, 1)
            pe.wait_ge(s_blk, 1)
            pe.wait_ge(s_w2, 16)

            def transpose_block(k, u, loads):
                pe.wait_ge(s_xin[u % U], 16 * loads)
                tr(XT[u % 2][:, 0:P], xin[u % U][:, H2:H2 + D], ident).then_inc(s_bt, 1)

            def hidden(k, u):
                pe.wait_ge(s_fc, k + 1)
                pe.wait_ge(s_bT, k + 1)
                for c in range(FC):
                    ins = mm(HID[u % R4][:, c * P:(c + 1) * P], firsts_c[u % R4][:, c * P:(c + 1) * P], xT[u % 2][:],
                             start=True, stop=True)
                ins.then_inc(s_hid, 1)

            def second(k, u, early=False):
                e = pe.value_load(blk_e[0:1, bass.ds(k, 1)], min_val=0, max_val=E - 1)
                pe.wait_ge(s_gelu, k + 1)
                if not early:
                    pe.wait_ge(s_yst, 2 * k - 3)
                for c in range(FC):
                    ins = mm(Y[u % 2][:, 0:D], g[u % R4][:, c * P:(c + 1) * P], w2sb[:, bass.ds(e * DFF + c * D, D)],
                             start=(c == 0), stop=(c == FC - 1))
                ins.then_inc(s_y, 1)

            def turn(i, first=False, last=False):
                for u in range(U):
                    k = i * U + u
                    if not (last and u == U - 1):
                        transpose_block(k + 1, u + 1, i + 1 + (u + 1) // U)
                    hidden(k, u)
                    if not (first and u < 2):
                        second(k - 2, (u - 2) % U, early=first and u < 4)

            transpose_block(0, 0, 1)
            turn(0, first=True)
            with pe.Fori(1, NBLK // U - 1) as i:
                turn(i)
            turn(NBLK // U - 1, last=True)
            for u in range(2):
                second(NBLK - 2 + u, U - 2 + u)


def program(nc, ins, outs):
    build(nc, *ins, *outs)


_OUT = (B, L, D)


def _constants():
    c = np.zeros((P, C_END), np.float32)
    p = np.arange(P)
    c[:, C_ID:C_ID + P] = np.eye(P)
    c[:, C_MASK:C_MASK + P] = (p[:, None] % CW) // DH == p[None, :] // M
    c[:, C_TRI:C_TRI + P] = p[:, None] < p[None, :]
    for r in range(64):
        head = r // DH
        c[64 + r, C_NORM + head * M:C_NORM + (head + 1) * M] = -1.0 / (2.0 * DH ** 0.5)
    c[:, C_PREF:C_PREF + E] = np.arange(E, 0, -1)
    c[:, C_LIST:C_LIST + E] = np.arange(E) * PITCH
    c[:, C_BLK:C_BLK + NBLK] = np.arange(NBLK)
    c[:, C_NUM:C_NUM + LT] = p[:, None] * LT + np.arange(LT)
    c[:, C_PAD] = NOROW + p
    return c


def kernel(L0_attn_x, L0_attn_Wq, L0_attn_bq, L0_attn_Wk, L0_attn_bk, L0_attn_Wv, L0_attn_bv, L0_attn_Wo,
           L0_attn_bo, L0_attn_orf, L0_ffn_gate_W, L0_ffn_gate_b, L0_ffn_W1, L0_ffn_b1, L0_ffn_W2, L0_ffn_b2,
           L0_c, L0_wmod):
    import concourse.bacc as bacc
    from concourse.bass_utils import run_bass_kernel_spmd

    a = lambda t: np.asarray(t)
    w = np.zeros((P, W_END), np.float32)
    wq, wk = a(L0_attn_Wq).T, a(L0_attn_Wk).T
    bq, bk = a(L0_attn_bq), a(L0_attn_bk)
    for n, (m, bias) in enumerate(((wq, bq), (wk, bk))):
        for half in range(2):
            cols, at = slice(64 * half, 64 * half + 64), (2 * n + half) * P
            w[:, at:at + 64] = m[:, cols]
            w[:, at + 64:at + P] = m[:, cols]
            w[0:64, W_BIAS + 2 * n + half] = bias[cols]
            w[64:, W_BIAS + 2 * n + half] = bias[cols]
    w[:, W_V:W_V + D] = a(L0_attn_Wv).T
    w[:, W_O:W_O + D] = a(L0_attn_Wo).T
    for head in range(64 // DH):
        w[head * DH:(head + 1) * DH, W_ORF + head * M:W_ORF + (head + 1) * M] = a(L0_attn_orf).T
    w[:, W_GATE:W_GATE + E] = a(L0_ffn_gate_W)
    w[:, W_CT:W_CT + B] = a(L0_c).T
    rows = np.concatenate([a(L0_attn_bv), a(L0_attn_bo), a(L0_ffn_gate_b)])
    rows = np.ascontiguousarray(np.broadcast_to(rows, (P, R_END)))

    firsts = np.zeros((P, E, WB), np.float32)
    firsts[:, :, 0:DFF] = a(L0_ffn_W1).transpose(1, 0, 2)
    firsts[:, :, WB2:WB2 + D] = a(L0_ffn_b2)
    firsts[:, :, WB1:WB] = a(L0_ffn_b1).reshape(E, FC, P).transpose(2, 0, 1)

    ins = {"x": a(L0_attn_x), "weights": w, "consts": _constants(), "rows": rows, "wmod": a(L0_wmod),
           "firsts": firsts.reshape(P, E * WB),
           "w2": a(L0_ffn_W2)}
    nc = bacc.Bacc("TRN2", target_bir_lowering=False, num_devices=1)
    arrays = {f"in_{n}": np.ascontiguousarray(v) for n, v in ins.items()}
    aps = [nc.dram_tensor(n, v.shape, mybir.dt.from_np(v.dtype), kind="ExternalInput").ap()
           for n, v in arrays.items()]
    out = nc.dram_tensor("out", _OUT, F32, kind="ExternalOutput").ap()
    program(nc, aps, [out])
    r = run_bass_kernel_spmd(nc, [arrays], core_ids=[0])
    return r.results[0]["out"]
```

```python
from contextlib import ExitStack

import numpy as np

import concourse.bass as bass
from concourse import mybir

F32 = mybir.dt.float32
BF16 = mybir.dt.bfloat16
F32R = mybir.dt.float32r
I32 = mybir.dt.int32
ACT = mybir.ActivationFunctionType
ALU = mybir.AluOpType
AX = mybir.AxisListType

B, L, D = 16, 512, 128
NH, DH, M = 16, 8, 32
E, DFF = 8, 512
P = 128
LT = L // P
NT = B * LT
NC = NH * M // P
CW = D // NC
FC = DFF // P
NBLK = NT + E - 1
U = 8
R4 = 4
TURNS = -(-NBLK // U)
REST = NBLK - (TURNS - 1) * U
DVE_ADDS = 4
KNOWN = B - 3
EARLY = (KNOWN * L - E * (P - 1) + P - 1) // P // U * U
PITCH = NT * P + P
PADROW = E * PITCH
H2, X2, GT, ID, PW = 0, D, 2 * D, 3 * D, 3 * D + 8
NOROW = 1 << 20
FEPS = 1e-6
LNEPS = 1e-5
GMIN = 0.25
WB1, WB2 = DFF, DFF + FC
WB = WB2 + D
KP = P + 2
ROWS = 4
GA, SB, CB, GB = range(ROWS)

W_KA, W_KB, W_QA, W_QB, W_V, W_O = (i * P for i in range(6))
W_ORF = 6 * P
W_GATE = W_ORF + 2 * P
W_BIAS = W_GATE + CW
W_CT = W_BIAS + 4
W_END = W_CT + B
C_ID, C_MASK, C_TRI, C_NORM = 0, P, 2 * P, 3 * P
C_PREF = C_NORM + 2 * P
C_LIST = C_PREF + E
C_NUM = C_LIST + E
C_PAD = C_NUM + LT
C_P = C_PAD + 1
C_END = C_P + 1
R_BV, R_BO, R_GB = 0, D, 2 * D
R_END = R_GB + E


class Batch:

    def __init__(self, i, r):
        self.i, self.r = i, r
        self.v, self.half, self.par = 2 * i + r, i + r // 2, r % 2

    def __add__(self, n):
        return Batch(self.i, self.r + n)


def over_batches(eng, batch):
    batch(Batch(0, 0), first=True)
    batch(Batch(0, 1), second=True)
    batch(Batch(0, 2))
    with eng.Fori(1, B // 2 - 2) as i:
        batch(Batch(i, 1))
        batch(Batch(i, 2))
    batch(Batch(B // 2 - 2, 1))
    batch(Batch(B // 2 - 2, 2), ahead=False)
    batch(Batch(B // 2 - 1, 1), ahead=False, last=True)


class Steps:

    def __init__(self, eng, sem, base):
        self.eng, self.sem, self.base, self.n = eng, sem, base, 0

    def mark(self, instruction):
        instruction.then_inc(self.sem, 1)
        self.n += 1

    def wait(self):
        self.eng.wait_ge(self.sem, self.base + self.n)


def build(nc, x, weights, consts, rows, wmod, firsts, w2, out):
    lists = nc.dram_tensor("experts_lists", [PADROW + P, PW], F32).ap()
    mods = nc.dram_tensor("modulation_rows", [B, ROWS * D], F32).ap()

    with ExitStack() as ctx:
        def sb(name, shape, dt=F32):
            return ctx.enter_context(nc.sbuf_tensor(name, shape, dt))

        def pb(name):
            return ctx.enter_context(nc.psum_tensor(name, [P, 512], F32))

        def sem(name):
            return ctx.enter_context(nc.semaphore(name))

        xall = sb("xall", [P, NT, D])
        modb = sb("modb", [P, B, ROWS, D])
        wsb = sb("wsb", [P, W_END])
        csb = sb("csb", [P, C_END])
        rsb = sb("rsb", [P, R_END])
        firsts_sb = sb("firsts_sb", [P, E * WB])
        w2sb = sb("w2sb", [P, E * DFF])
        feat_w = sb("feat_w", [P, 2 * P])
        ones32 = sb("ones32", [P, CW])
        mhalf = sb("mhalf", [P, LT])
        padding = sb("padding", [P, PW])
        qf = sb("qf", [P, NC, L])
        wmod_sb = qf[:, :, :].rearrange("p c l -> p (c l)")[:, 0:6 * D]
        silu = sb("silu", [P, 3, B])
        modrow = sb("modrow", [B, ROWS, D])
        gsign = sb("gsign", [B, 2, D])
        ca1 = sb("ca1", [P, B])
        sa = sb("sa", [P, B])
        st1 = sb("st1", [P, LT, 6])
        mv1 = sb("mv1", [P, LT, 3])
        ve1 = sb("ve1", [P, LT])
        rstd1 = sb("rstd1", [P, LT])
        st2 = sb("st2", [P, LT, 6])
        mv2 = sb("mv2", [P, LT, 3])
        ve2 = sb("ve2", [P, LT])
        rstd2 = sb("rstd2", [P, LT])
        shared = sb("shared", [P, max(R4 * WB2, 5 * L)])
        xn1_, hT_, stack0_, stack1_, v_ = (shared[:, n * L:(n + 1) * L] for n in range(5))
        xn1, v_sb = (r.rearrange("p (t d) -> p t d", t=LT) for r in (xn1_, v_))
        xn2 = sb("xn2", [P, LT, D])
        hT = hT_
        hT_hi = sb("hT_hi", [P, L], F32R)
        hT_lo = sb("hT_lo", [P, L], F32R)
        w_hi = sb("w_hi", [P, 4 * P], F32R)
        w_lo = sb("w_lo", [P, 4 * P], F32R)
        q_hi = sb("q_hi", [P, 2, L], F32R)
        q_lo = sb("q_lo", [P, 2, L], F32R)
        fw_hi = sb("fw_hi", [P, 2 * P], F32R)
        fw_lo = sb("fw_lo", [P, 2 * P], F32R)
        stack = [stack0_, stack1_, sb("stack2", [P, L]), sb("stack3", [P, L])]
        kf = sb("kf", [P, LT, NC, KP])
        kvT = sb("kvT", [P, 2 * P])
        kvsum = sb("kvsum", [P, 2])
        kveps = sb("kveps", [P, 2])
        kvm = sb("kvm", [P, 2 * P])
        den = sb("den", [P, L])
        rden = sb("rden", [P, L])
        oT = sb("oT", [P, L])
        wo = sb("wo", [P, D])
        bog = sb("bog", [P, D])
        pay = [sb(f"pay{n}", [P, LT, PW]) for n in range(2)]
        h2T = sb("h2T", [P, L])
        lgT = sb("lgT", [P, P])
        tri = sb("tri", [P, P], BF16)
        ones_bf = sb("ones_bf", [P, P], BF16)
        lg = sb("lg", [P, LT, E])
        top = sb("top", [P, LT])
        eq = sb("eq", [P, LT, E])
        oh = sb("oh", [P, LT, E], BF16)
        seen = sb("seen", [P, E], BF16)
        ohsum = sb("ohsum", [P, E])
        rk = sb("rk", [P, LT, E])
        slot_f = sb("slot_f", [P, LT])
        slot = [sb(f"slot{n}", [P, LT], I32) for n in range(2)]
        num = sb("num", [P, LT])
        cnt_i = sb("cnt_i", [P, E], I32)
        cnt_b = sb("cnt_b", [P, E], I32)
        nblk = sb("nblk", [P, E])
        endblk = sb("endblk", [P, E])
        done = sb("done", [P, E + 1])
        jump = sb("jump", [P, E])
        tab = sb("tab", [P, 2])
        tmp = sb("tmp", [P, 2, E])
        blk_e = sb("blk_e", [P, NBLK], I32)
        blk_row = sb("blk_row", [P, NBLK], I32)
        xin = [sb(f"xin{u}", [P, PW]) for u in range(U)]
        xT = [sb(f"xT{u}", [P, P]) for u in range(2)]
        firsts_c = [shared[:, u * WB2:(u + 1) * WB2] for u in range(R4)]
        g = [qf[:, u, :] for u in range(R4)]
        kf_row = kf[:, :, :, :].rearrange("p t c k -> p (t c k)")
        yb = [kf_row[:, u * D:(u + 1) * D] for u in range(U)]
        b2c = [kf_row[:, (U + u) * D:(U + u + 1) * D] for u in range(U)]
        ids = [sb(f"ids{u}", [P, 1], I32) for u in range(U)]

        F = [pb("ps_feat0"), pb("ps_feat1")]
        KV, G = pb("ps_kv"), pb("ps_den")
        H, I = pb("ps_out"), pb("ps_gate")
        PJ = [pb("ps_proj0"), pb("ps_proj1")]
        HID = [F[0], F[1], KV, G]
        XT = H
        Y = PJ

        ident = csb[:, C_ID:C_ID + P]
        mask = csb[:, C_MASK:C_MASK + P]

        s_w = sem("weights_in")
        s_c = sem("consts_in")
        s_r = sem("rows_in")
        s_wm = sem("wmod_in")
        s_w1 = sem("w1_in")
        s_w2 = sem("w2_in")
        s_x = [sem("x_in_even"), sem("x_in_odd")]
        s_mrow = sem("mod_rows_out")
        s_mb = sem("mod_rows_in")
        s_set = sem("setup_step")
        s_pset = sem("pool_setup")
        s_fw = sem("feature_weights")
        s_silue = sem("silu_exp")
        s_silu = sem("silu_ready")
        s_modp = sem("mod_products")
        s_modr = sem("mod_rows_ready")
        s_cols = sem("mod_columns_ready")
        s_pad = sem("padding_out")
        s_ln1 = sem("ln1_step")
        s_ln2 = sem("ln2_step")
        s_var1 = sem("var1_ready")
        s_var2 = sem("var2_ready")
        s_rstd1 = sem("rstd1_ready")
        s_rstd2 = sem("rstd2_ready")
        s_xn1 = sem("xn1_ready")
        s_xn2 = sem("xn2_ready")
        s_t1 = sem("xn1_transposed")
        s_hT = sem("hT_ready")
        s_hi = sem("hT_hi_ready")
        s_lo = sem("hT_lo_ready")
        s_qhi = sem("q_hi_ready")
        s_qlo = sem("q_lo_ready")
        s_whi = sem("weights_hi_ready")
        s_wlo = sem("weights_lo_ready")
        s_proj = sem("projections")
        s_kval = sem("k_values")
        s_qv = sem("q_values")
        s_sq = sem("stack_squares")
        s_v = sem("v_ready")
        s_feat = sem("feature_products")
        s_exp = sem("features_ready")
        s_kv = sem("kv_product")
        s_kvT = sem("kvT_ready")
        s_kvt = sem("kv_transposed")
        s_kvm = sem("kvm_ready")
        s_eps = sem("kveps_ready")
        s_den = sem("den_product")
        s_num = sem("num_product")
        s_denp = sem("den_ready")
        s_rden = sem("rden_ready")
        s_oT = sem("oT_ready")
        s_wo = sem("wo_ready")
        s_bog = sem("bog_ready")
        s_xb = sem("xb_ready")
        s_op = sem("out_product")
        s_x2 = sem("x2_ready")
        s_h2m = sem("h2_scaled")
        s_h2 = sem("h2_ready")
        s_h2t = sem("h2_transposed")
        s_h2T = sem("h2T_ready")
        s_gb = sem("gate_rows_ready")
        s_lg = sem("gate_product")
        s_lgT = sem("gateT_ready")
        s_lgt = sem("gate_transposed")
        s_rt = sem("routing_step")
        s_oh = sem("onehot_ready")
        s_rank = sem("rank_products")
        s_seen = sem("seen_updated")
        s_slot = sem("slots_ready")
        s_scat = [sem("rows_scattered_even"), sem("rows_scattered_odd")]
        s_end = sem("table_step")
        s_cnt = sem("count_product")
        s_tab = sem("table_columns")
        s_tabT = sem("table_transposed")
        s_cnti = sem("counts_ready")
        s_blk = sem("block_table_ready")
        s_xin = [sem(f"block_in{u}") for u in range(U)]
        s_bt = sem("block_transposed")
        s_bT = sem("block_T_ready")
        s_fc = sem("firsts_copied")
        s_b2 = sem("b2_copied")
        s_hid = sem("hidden_product")
        s_gelu = sem("hidden_ready")
        s_y = sem("result_product")
        s_yb = sem("result_ready")
        s_yst = sem("result_step")
        s_yout = [sem(f"result_out{u}") for u in range(U)]

        block = ctx.enter_context(nc.Block())

        def apart(eng):
            eng.wait_ge(s_w, 16)

        def snapped(eng, value):
            return value if isinstance(value, int) else eng.snap(value)

        @block.sync
        def _(sp):
            sp.dma_start(wsb[:], weights).then_inc(s_w, 16)
            sp.dma_start(wmod_sb, wmod).then_inc(s_wm, 16)
            sp.dma_start(csb[:], consts).then_inc(s_c, 16)
            xv = x.rearrange("b (p t) d -> b p t d", t=LT)

            def load_x(b, parity):
                sp.dma_start(xall[:, bass.ds(b * LT, LT), :], xv[bass.ds(b, 1), :, :, :])\
                    .then_inc(s_x[parity], 16)

            load_x(0, 0)
            load_x(1, 1)
            sp.dma_start(rsb[:], rows).then_inc(s_r, 16)
            sp.wait_ge(s_modr, 1)
            sp.dma_start(mods, modrow[:, :, :].rearrange("b r d -> b (r d)")).then_inc(s_mrow, 16)
            sp.wait_ge(s_mrow, 16)
            sp.dma_start(modb[:, :, :, :].rearrange("p b r d -> p (b r d)"),
                         mods.rearrange("b n -> (b n)").unsqueeze(0).to_broadcast([P, B * ROWS * D]))\
                .then_inc(s_mb, 16)
            with sp.Fori(1, B // 2) as i:
                for parity in range(2):
                    sp.wait_ge(s_x[parity], 16 * i)
                    load_x(2 * i + parity, parity)
            sp.dma_start(firsts_sb[:], firsts).then_inc(s_w1, 16)
            sp.dma_start(w2sb[:, :].rearrange("p (e c d) -> p e c d", e=E, c=FC),
                         w2.rearrange("e (c p) d -> p e c d", p=P)).then_inc(s_w2, 16)
            sp.wait_ge(s_pset, 5)
            sp.dma_start(lists[PADROW:PADROW + P, :], padding[:]).then_inc(s_pad, 16)

            def load_block(k, u):
                row = sp.value_load(blk_row[0:1, bass.ds(k, 1)], min_val=0, max_val=PADROW)
                sp.dma_start(xin[u][:], lists[bass.ds(row, P), :]).then_inc(s_xin[u], 16)

            def load_next(i, u):
                sp.wait_ge(s_yb, i * U + (u + 1))
                load_block(i * U + (U + u), u)

            def load_turns(start, stop):
                with sp.Fori(start, stop) as i:
                    for u in range(U):
                        load_next(i, u)

            for n in range(2):
                sp.wait_ge(s_scat[n], 16 * LT * ((KNOWN + 1 - n) // 2))
            sp.wait_ge(s_blk, 1)
            for u in range(U):
                load_block(u, u)
            load_turns(0, 2)
            sp.wait_ge(s_cnti, 1)
            for e in range(E):
                load_next(2, e)
                count = sp.value_load(cnt_i[0:1, e:e + 1], min_val=0, max_val=NT * P)
                sp.dma_start(lists[bass.ds(count + e * PITCH, P), :], padding[:]).then_inc(s_pad, 16)
            load_turns(3, EARLY // U - 1)
            for n in range(2):
                sp.wait_ge(s_scat[n], 16 * LT * B // 2)
            sp.wait_ge(s_pad, 16 * (E + 1))
            sp.wait_ge(s_blk, 2)
            load_turns(EARLY // U - 1, TURNS - 2)
            for u in range(REST):
                load_next(TURNS - 2, u)

        @block.gpsimd
        def _(pool):
            g_ = nc.gpsimd
            g_.memset(mhalf[:], -0.5).then_inc(s_pset, 1)
            g_.memset(padding[:], 0.0).then_inc(s_pset, 1)
            for n in range(2):
                g_.memset(pay[n][:, :, ID:PW], 0.0).then_inc(s_pset, 1)

            pool.wait_ge(s_w, 16)
            g_.tensor_copy(w_hi[:], wsb[:, 0:4 * P]).then_inc(s_whi, 1)
            pool.wait_ge(s_whi, 1)
            g_.tensor_tensor(w_lo[:], wsb[:, 0:4 * P], w_hi[:], ALU.subtract).then_inc(s_wlo, 1)
            pool.wait_ge(s_fw, 3)
            g_.tensor_copy(fw_hi[:], feat_w[:]).then_inc(s_whi, 1)
            pool.wait_ge(s_whi, 2)
            g_.tensor_tensor(fw_lo[:], feat_w[:], fw_hi[:], ALU.subtract).then_inc(s_wlo, 1)

            def rstd(b, which):
                ve, out_, ready, done = ((ve1, rstd1, s_var1, s_rstd1), (ve2, rstd2, s_var2, s_rstd2))[which]
                pool.wait_ge(ready, b.v + 1)
                g_.tensor_tensor(out_[:], ve[:], mhalf[:], ALU.pow).then_inc(done, 1)

            def gated(b, first=False):
                ga = modb[:, bass.ds(b.v, 1), GA, :]
                if not first:
                    apart(pool)
                    pool.wait_ge(s_xb, b.v)
                g_.tensor_tensor(bog[:], rsb[:, R_BO:R_BO + D], ga.squeeze(1), ALU.mult).then_inc(s_bog, 1)
                apart(pool)
                pool.wait_ge(s_bog, b.v + 1)
                pool.wait_ge(s_xn1, b.v + 1)
                xt = xall[:, bass.ds(b.v * LT, LT), :]
                g_.tensor_tensor(xt, xt, bog[:, :].unsqueeze(1).to_broadcast([P, LT, D]), ALU.add)\
                    .then_inc(s_xb, 1)
                if not first:
                    apart(pool)
                    pool.wait_ge(s_op, b.v)
                g_.tensor_tensor(wo[:], wsb[:, W_O:W_O + D], ga.squeeze(1), ALU.mult).then_inc(s_wo, 1)

            def experts_input(b):
                h2 = pay[b.par][:, :, H2:H2 + D]
                apart(pool)
                pool.wait_ge(s_xn2, b.v + 1)
                g_.tensor_tensor(h2, xn2[:], modb[:, bass.ds(b.v, 1), CB, :].to_broadcast([P, LT, D]), ALU.mult)\
                    .then_inc(s_h2m, 1)
                apart(pool)
                pool.wait_ge(s_h2m, b.v + 1)
                g_.tensor_tensor(h2, h2, modb[:, bass.ds(b.v, 1), SB, :].to_broadcast([P, LT, D]), ALU.add)\
                    .then_inc(s_h2, 1)

            def scatter(b, tiles=range(LT)):
                value = snapped(pool, b.v + 1)
                apart(pool)
                pool.wait_ge(s_slot, value)
                pool.wait_ge(s_gb, value)
                for t in tiles:
                    g_.indirect_dma_start(out=lists, in_=pay[b.par][:, t, :], in_offset=None,
                                          out_offset=bass.IndirectOffsetOnAxis(ap=slot[b.par][:, t:t + 1], axis=0))\
                        .then_inc(s_scat[b.par], 16)

            def batch(b, first=False, second=False, last=False, ahead=True):
                if first:
                    pool.wait_ge(s_r, 16)
                    pool.wait_ge(s_mb, 16)
                gated(b, first)
                if not first:
                    rstd(b + -1, 1)
                    experts_input(b + -1)
                if ahead:
                    rstd(b + 2, 0)
                if not first and not second:
                    scatter(b + -2)

            rstd(Batch(0, 0), 0)
            rstd(Batch(0, 1), 0)
            over_batches(pool, batch)
            end = Batch(0, B)
            scatter(end + -2)

            rows_out = out.rearrange("b l d -> (b l) d")
            last_row = pool.to_reg(B * L - 1)

            def add(k, u):
                value = pool.to_reg(2 * k + 2)
                apart(pool)
                pool.wait_ge(s_yst, value)
                g_.tensor_tensor(yb[u], yb[u], xin[u][:, X2:X2 + D], ALU.add).then_inc(s_yb, 1)

            def store(k, u):
                value = pool.to_reg(k + 1)
                apart(pool)
                pool.wait_ge(s_yb, value)
                g_.indirect_dma_start(out=rows_out, in_=yb[u], in_offset=None,
                                      out_offset=bass.IndirectOffsetOnAxis(ap=ids[u][:, 0:1], axis=0),
                                      bounds_check=last_row, oob_is_err=False).then_inc(s_yout[u], 16)

            between = {1: lambda: rstd(end + -1, 1), 3: lambda: experts_input(end + -1)}
            for t in range(LT):
                between[U + 2 + t] = lambda t=t: scatter(end + -1, [t])
            for k in range(2 * U):
                if k >= DVE_ADDS:
                    add(k, k % U)
                store(k, k % U)
                if k in between:
                    between[k]()
            with pool.Fori(2, TURNS - 1) as i:
                for u in range(U):
                    add(i * U + u, u)
                    store(i * U + u, u)
            for u in range(REST):
                add((TURNS - 1) * U + u, u)
                store((TURNS - 1) * U + u, u)
            for u in range(U):
                pool.wait_ge(s_yout[u], 16 * (TURNS if u < REST else TURNS - 1))

        @block.scalar
        def _(act):
            a = nc.scalar
            act.wait_ge(s_w, 16)
            a.activation(silu[:, 0, :], wsb[:, W_CT:W_CT + B], ACT.Exp, scale=-1.0).then_inc(s_silue, 1)

            def squares(b, i):
                act.wait_ge(s_proj, 5 * b.v + i + 1)
                a.activation(stack[i][64:128, :], PJ[i % 2][64:128, :], ACT.Square,
                             bias=wsb[64:128, W_BIAS + i:W_BIAS + i + 1]).then_inc(s_sq, 1)

            def values(b, i):
                a.activation(stack[i][0:64, :], PJ[i % 2][0:64, :], ACT.Identity,
                             bias=wsb[0:64, W_BIAS + i:W_BIAS + i + 1]).then_inc(s_kval if i < 2 else s_qv, 1)

            def hT_high(b):
                act.wait_ge(s_hT, b.v + 1)
                a.activation(hT_hi[:], hT[:], ACT.Copy).then_inc(s_hi, 1)

            def q_high(b, n):
                act.wait_ge(s_qv, 2 * b.v + n + 1)
                a.activation(q_hi[:, n, :], stack[2 + n][:], ACT.Copy).then_inc(s_qhi, 1)

            def feature(b, j):
                act.wait_ge(s_feat, 2 * NC * b.v + j + 1)
                src = F[j % 2][:, :]
                if j < LT:
                    dst, src = kf[:, j, :, 0:P], src.rearrange("p (c m) -> p c m", c=NC)
                else:
                    dst = qf[:, j - LT, :]
                a.activation(dst, src, ACT.Exp).then_inc(s_exp, 1)

            def h2T_copy(b):
                act.wait_ge(s_h2t, b.v + 1)
                a.activation(h2T[:], I[:], ACT.Copy).then_inc(s_h2T, 1)

            def gateT(b):
                act.wait_ge(s_lg, b.v + 1)
                a.activation(lgT[:], I[:, 0:P], ACT.Copy).then_inc(s_lgT, 1)

            def gate_rows(b):
                if not (isinstance(b.half, int) and b.half == 0):
                    value = snapped(act, 16 * LT * b.half)
                    apart(act)
                    act.wait_ge(s_scat[b.par], value)
                a.activation(pay[b.par][:, :, GT:GT + D],
                             modb[:, bass.ds(b.v, 1), GB, :].to_broadcast([P, LT, D]), ACT.Copy).then_inc(s_gb, 1)

            def batch(b, first=False, second=False, last=False, ahead=True):
                for j in range(2 * NC):
                    if j == 2 * NC - 2 and not last:
                        hT_high(b + 1)
                    feature(b, j)
                    if j == 1:
                        q_high(b, 0)
                        q_high(b, 1)
                act.wait_ge(s_kvt, b.v + 1)
                a.activation(kvm[:], G[:, 0:2 * P], ACT.Copy).then_inc(s_kvm, 1)
                if not last:
                    squares(b + 1, 0)
                    values(b + 1, 0)
                    squares(b + 1, 1)
                    values(b + 1, 1)
                act.wait_ge(s_den, b.v + 1)
                act.wait_ge(s_eps, b.v + 1)
                a.activation(den[:], G[:], ACT.Identity, bias=kveps[:, 1:2]).then_inc(s_denp, 1)
                if not first:
                    h2T_copy(b + -1)
                if not last:
                    for n in (2, 3):
                        squares(b + 1, n)
                        values(b + 1, n)
                if first:
                    act.wait_ge(s_mb, 16)
                if not first:
                    gateT(b + -1)
                    gate_rows(b + -1)

            hT_high(Batch(0, 0))
            for n in range(4):
                squares(Batch(0, 0), n)
                values(Batch(0, 0), n)
            over_batches(act, batch)
            end = Batch(0, B)

            def copy_xT(k, u):
                act.wait_ge(s_bt, k + 1)
                a.activation(xT[u % 2][:], XT[:, 0:P], ACT.Copy).then_inc(s_bT, 1)

            def turn(i, last=False, between={}):
                for u in range(REST if last else U):
                    if not (last and u == REST - 1):
                        copy_xT(i * U + (u + 1), u + 1)
                    act.wait_ge(s_hid, i * U + (u + 1))
                    for c in range(FC):
                        ins = a.activation(g[u % R4][:, c * P:(c + 1) * P], HID[u % R4][:, c * P:(c + 1) * P],
                                           ACT.Gelu, bias=firsts_c[u % R4][:, WB1 + c:WB1 + c + 1])
                    ins.then_inc(s_gelu, 1)
                    for step in between.get(u, []):
                        step()

            copy_xT(0, 0)
            turn(0)
            turn(1, between={
                1: [lambda: h2T_copy(end + -1), lambda: gate_rows(end + -1)],
                2: [lambda: gateT(end + -1)]})
            with act.Fori(2, TURNS - 1) as i:
                turn(i)
            turn(TURNS - 1, last=True)

        @block.vector
        def _(dve):
            v = nc.vector

            def stats(b, which):
                st, mv, ve, step, ready = ((st1, mv1, ve1, s_ln1, s_var1), (st2, mv2, ve2, s_ln2, s_var2))[which]
                s = Steps(dve, step, 3 * b.v)
                for t in range(LT):
                    ins = v.bn_stats(st[:, t, :], ln_row(b, which, t))
                s.mark(ins)
                s.wait()
                v.tensor_tensor(mv[:, :, 0:2], st[:, :, 1:3], st[:, :, 4:6], ALU.add)
                s.mark(v.tensor_tensor(mv[:, :, 2], st[:, :, 1], st[:, :, 4], ALU.subtract))
                s.wait()
                v.tensor_scalar(mv[:, :, 0], mv[:, :, 0], 0.5, None, ALU.mult)
                v.tensor_scalar(mv[:, :, 1], mv[:, :, 1], 1.0 / D, LNEPS, ALU.mult, ALU.add)
                s.mark(v.tensor_tensor(mv[:, :, 2], mv[:, :, 2], mv[:, :, 2], ALU.mult))
                s.wait()
                v.scalar_tensor_tensor(out=ve[:], in0=mv[:, :, 2], scalar=0.25, in1=mv[:, :, 1],
                                       op0=ALU.mult, op1=ALU.add).then_inc(ready, 1)

            def ln_row(b, which, t):
                if which:
                    return pay[b.par][:, t, X2:X2 + D]
                return xall[:, bass.ds(b.v * LT + t, 1), :].squeeze(1)

            def first_stats(b):
                value = snapped(dve, 16 * (b.half + 1))
                apart(dve)
                dve.wait_ge(s_x[b.par], value)
                stats(b, 0)

            def normalise(b, which, first=False):
                mv, rstd, xn, rdy, done = ((mv1, rstd1, xn1, s_rstd1, s_xn1), (mv2, rstd2, xn2, s_rstd2, s_xn2))[which]
                dve.wait_ge(rdy, b.v + 1)
                if not first:
                    dve.wait_ge(s_h2m if which else s_t1, b.v)
                for t in range(LT):
                    ins = v.tensor_scalar(xn[:, t, :], ln_row(b, which, t), mv[:, t, 0:1], rstd[:, t:t + 1],
                                          ALU.subtract, ALU.mult)
                ins.then_inc(done, 1)

            def modulate(b):
                dve.wait_ge(s_t1, b.v + 1)
                v.tensor_scalar(hT[:], H[:], ca1[:, bass.ds(b.v, 1)], sa[:, bass.ds(b.v, 1)], ALU.mult, ALU.add)\
                    .then_inc(s_hT, 1)

            def hT_low(b):
                dve.wait_ge(s_hi, b.v + 1)
                v.tensor_tensor(hT_lo[:], hT[:], hT_hi[:], ALU.subtract).then_inc(s_lo, 1)

            v.memset(ones32[:], 1.0).then_inc(s_set, 1)
            v.memset(kf[:, :, :, P:KP], FEPS).then_inc(s_set, 1)
            v.memset(ones_bf[:], 1.0).then_inc(s_set, 1)
            v.memset(seen[:], 0.0).then_inc(s_set, 1)
            dve.wait_ge(s_silue, 1)
            v.tensor_scalar(silu[:, 1, :], silu[:, 0, :], 1.0, None, ALU.add).then_inc(s_set, 1)
            dve.wait_ge(s_set, 5)
            v.reciprocal(silu[:, 2, :], silu[:, 1, :]).then_inc(s_set, 1)
            dve.wait_ge(s_set, 6)
            v.tensor_tensor(silu[:, 0, :], silu[:, 2, :], wsb[:, W_CT:W_CT + B], ALU.mult).then_inc(s_silu, 1)
            dve.wait_ge(s_c, 16)
            v.tensor_copy(num[:], csb[:, C_NUM:C_NUM + LT]).then_inc(s_fw, 1)
            dve.wait_ge(s_pset, 4)
            v.tensor_copy(padding[:, ID:ID + 1].bitcast(I32), csb[:, C_PAD:C_PAD + 1]).then_inc(s_pset, 1)
            v.scalar_tensor_tensor(out=feat_w[:], in0=wsb[:, W_ORF:W_ORF + 2 * P], scalar=float(DH ** -0.25),
                                   in1=csb[:, C_NORM:C_NORM + 2 * P], op0=ALU.mult, op1=ALU.add).then_inc(s_fw, 1)
            v.tensor_copy(tri[:], csb[:, C_TRI:C_TRI + P]).then_inc(s_fw, 1)
            first_stats(Batch(0, 0))
            dve.wait_ge(s_modp, 1)
            v.tensor_copy(sa[:], F[0][:, 0:B])
            v.tensor_scalar(ca1[:], F[0][:, B:2 * B], 1.0, None, ALU.add).then_inc(s_cols, 1)
            normalise(Batch(0, 0), 0, first=True)
            v.tensor_copy(modrow[:, SB, :], G[0:B, 0:D])
            v.tensor_scalar(modrow[:, CB, :], G[0:B, D:2 * D], 1.0, None, ALU.add)
            gates = [(n, row, src[0:B, 2 * D:3 * D]) for n, (row, src) in enumerate(((GA, KV), (GB, G)))]
            for n, row, gate in gates:
                ins = v.tensor_scalar(gsign[:, n, :], gate, 0.0, 2.0, ALU.is_ge, ALU.mult)
            ins.then_inc(s_set, 1)
            dve.wait_ge(s_set, 7)
            v.tensor_scalar(gsign[:, :, :], gsign[:, :, :], -1.0, None, ALU.add).then_inc(s_set, 1)
            dve.wait_ge(s_cols, 1)
            modulate(Batch(0, 0))
            dve.wait_ge(s_set, 8)
            for n, row, gate in gates:
                ins = v.tensor_tensor(modrow[:, row, :], gate, gsign[:, n, :], ALU.mult)
            ins.then_inc(s_set, 1)
            hT_low(Batch(0, 0))
            dve.wait_ge(s_set, 9)
            for n, row, gate in gates:
                ins = v.scalar_tensor_tensor(out=modrow[:, row, :], in0=modrow[:, row, :], scalar=GMIN,
                                             in1=gsign[:, n, :], op0=ALU.max, op1=ALU.mult)
            ins.then_inc(s_modr, 1)

            def q_low(b, n):
                dve.wait_ge(s_qhi, 2 * b.v + n + 1)
                v.tensor_tensor(q_lo[:, n, :], stack[2 + n][:], q_hi[:, n, :], ALU.subtract).then_inc(s_qlo, 1)

            def v_values(b):
                dve.wait_ge(s_proj, 5 * b.v + 5)
                v.tensor_tensor(v_sb[:], PJ[0][:, :].rearrange("p (t d) -> p t d", t=LT),
                                rsb[:, R_BV:R_BV + D].unsqueeze(1).to_broadcast([P, LT, D]), ALU.add).then_inc(s_v, 1)

            def kv_values(b, first=False):
                dve.wait_ge(s_kv, b.v + 1)
                if not first:
                    dve.wait_ge(s_denp, b.v)
                v.scalar_tensor_tensor(out=kvT[:, 0:P], in0=KV[:, 0:P], scalar=KV[:, P:P + 1], in1=mask,
                                       op0=ALU.add, op1=ALU.mult, accum_out=kvsum[:, 0:1])
                v.scalar_tensor_tensor(out=kvT[:, P:2 * P], in0=KV[:, 256:256 + P], scalar=float(L * FEPS), in1=mask,
                                       op0=ALU.add, op1=ALU.mult, accum_out=kvsum[:, 1:2]).then_inc(s_kvT, 1)
                dve.wait_ge(s_kvT, b.v + 1)
                v.tensor_scalar(kveps[:], kvsum[:], FEPS, None, ALU.mult).then_inc(s_eps, 1)

            def attention(b):
                dve.wait_ge(s_denp, b.v + 1)
                v.reciprocal(rden[:], den[:]).then_inc(s_rden, 1)
                dve.wait_ge(s_rden, b.v + 1)
                dve.wait_ge(s_num, b.v + 1)
                v.scalar_tensor_tensor(out=oT[:], in0=KV[:], scalar=kveps[:, 0:1], in1=rden[:],
                                       op0=ALU.add, op1=ALU.mult).then_inc(s_oT, 1)

            def residual(b, bank=H):
                dve.wait_ge(s_op, b.v + 1)
                dve.wait_ge(s_xb, b.v + 1)
                if not (isinstance(b.half, int) and b.half == 0):
                    dve.wait_ge(s_scat[b.par], 16 * LT * b.half)
                v.tensor_tensor(pay[b.par][:, :, X2:X2 + D], bank[:, :].rearrange("p (t d) -> p t d", t=LT),
                                xall[:, bass.ds(b.v * LT, LT), :], ALU.add).then_inc(s_x2, 1)

            def second_stats(b):
                value = snapped(dve, b.v + 1)
                apart(dve)
                dve.wait_ge(s_x2, value)
                stats(b, 1)

            def experts(b):
                s = Steps(dve, s_rt, 8 * b.v)
                tb = lambda r: r.unsqueeze(1).to_broadcast([P, LT, E])
                eb = lambda r: r.unsqueeze(2).to_broadcast([P, LT, E])
                dve.wait_ge(s_lgt, b.v + 1)
                s.mark(v.tensor_tensor(lg[:], I[:, P:2 * P].rearrange("p (t c) -> p t c", t=LT)[:, :, 0:E],
                                       tb(rsb[:, R_GB:R_GB + E]), ALU.add))
                s.wait()
                s.mark(v.tensor_reduce(out=top[:], in_=lg[:], op=ALU.max, axis=AX.X))
                s.wait()
                s.mark(v.tensor_tensor(eq[:], lg[:], eb(top[:, :]), ALU.is_ge))
                s.wait()
                s.mark(v.tensor_tensor(eq[:], eq[:], tb(csb[:, C_PREF:C_PREF + E]), ALU.mult))
                s.wait()
                s.mark(v.tensor_reduce(out=top[:], in_=eq[:], op=ALU.max, axis=AX.X))
                s.wait()
                v.tensor_tensor(oh[:], eq[:], eb(top[:, :]), ALU.is_equal).then_inc(s_oh, 1)

            def slots(b):
                s = Steps(dve, s_rt, 8 * b.v + 5)
                dve.wait_ge(s_rank, b.v + 1)
                v.tensor_reduce(out=ohsum[:], in_=oh[:, :, :].rearrange("p t e -> p e t"), op=ALU.add, axis=AX.X)
                s.mark(v.tensor_tensor(rk[:], I[:, 2 * P:2 * P + LT * E].rearrange("p (t e) -> p t e", t=LT),
                                       csb[:, C_LIST:C_LIST + E].unsqueeze(1).to_broadcast([P, LT, E]), ALU.add))
                s.wait()
                v.tensor_tensor(seen[:], seen[:], ohsum[:], ALU.add).then_inc(s_seen, 1)
                v.tensor_copy(pay[b.par][:, :, ID:ID + 1].bitcast(I32), num[:, :].unsqueeze(2))
                s.mark(v.tensor_tensor(rk[:], rk[:], oh[:], ALU.mult))
                s.wait()
                v.tensor_scalar(num[:], num[:], float(L), None, ALU.add)
                s.mark(v.tensor_reduce(out=slot_f[:], in_=rk[:], op=ALU.add, axis=AX.X))
                s.wait()
                v.tensor_copy(slot[b.par][:], slot_f[:]).then_inc(s_slot, 1)

            counts = I[:, 2 * P + LT * E:2 * P + LT * E + E]

            def early_counts():
                dve.wait_ge(s_cnt, 1)
                dve.wait_ge(s_lgt, KNOWN + 1)
                v.tensor_copy(cnt_b[:], counts).then_inc(s_end, 1)
                steps[0] += 1

            def table(part):
                s = Steps(dve, s_end, steps[0])
                if part == 1:
                    dve.wait_ge(s_cnt, 2)
                    v.tensor_copy(cnt_i[:], counts).then_inc(s_cnti, 1)
                    s.mark(v.tensor_scalar(nblk[:], counts, float(P - 1), None, ALU.add))
                    s.wait()
                    s.mark(v.tensor_copy(cnt_b[:], nblk[:]))
                s.wait()
                s.mark(v.tensor_scalar(cnt_b[:], cnt_b[:], P.bit_length() - 1, None, ALU.arith_shift_right))
                s.wait()
                s.mark(v.tensor_copy(nblk[:], cnt_b[:]))
                s.wait()
                if part == 0:
                    s.mark(v.memset(done[:], 0.0))
                    s.wait()
                s.mark(v.tensor_tensor(nblk[:], nblk[:], done[:, 0:E], ALU.subtract))
                s.wait()
                v.scalar_tensor_tensor(out=jump[:], in0=nblk[:], scalar=-1.0, in1=done[:, 1:E + 1],
                                       op0=ALU.mult, op1=ALU.add)
                s.mark(v.tensor_tensor_scan(out=endblk[:], data0=ones32[:, 0:E], data1=nblk[:], initial=0.0,
                                            op0=ALU.mult, op1=ALU.add))
                s.wait()
                s.mark(v.tensor_tensor(jump[:], jump[:], done[:, 0:E], ALU.subtract))
                s.wait()
                s.mark(v.tensor_scalar(jump[:], jump[:], float(PITCH // P), None, ALU.add))
                s.wait()
                number = csb[:, C_P:C_P + 1]
                v.scalar_tensor_tensor(out=tmp[:, 0, :], in0=endblk[:], scalar=number, in1=ones32[:, 0:E],
                                       op0=ALU.is_le, op1=ALU.mult, accum_out=tab[:, 0:1])
                s.mark(v.scalar_tensor_tensor(out=tmp[:, 1, :], in0=endblk[:], scalar=number, in1=jump[:],
                                              op0=ALU.is_le, op1=ALU.mult, accum_out=tab[:, 1:2]))
                s.wait()
                v.tensor_scalar(tab[:, 0:1], tab[:, 0:1], float(E - 1), None, ALU.min)
                s.mark(v.tensor_scalar(tab[:, 1:2], tab[:, 1:2], number, done[:, 0:1], ALU.add, ALU.add))
                s.wait()
                v.tensor_scalar(tab[:, 1:2], tab[:, 1:2], float(P), float(PADROW), ALU.mult, ALU.min)\
                    .then_inc(s_tab, 1)
                if part == 0:
                    s.mark(v.tensor_scalar(endblk[:], endblk[:], float(EARLY), None, ALU.min))
                    dve.wait_ge(s_tab, 1)
                    s.wait()
                    v.tensor_copy(done[:, 0:1], endblk[:, 0:1])
                    s.mark(v.tensor_tensor(done[:, 1:E], endblk[:, 1:E], endblk[:, 0:E - 1], ALU.subtract))
                    s.wait()
                steps[0] += s.n

            def table_rows(part):
                at, n = (0, EARLY) if part == 0 else (EARLY, NBLK - EARLY)
                dve.wait_ge(s_tabT, part + 1)
                v.tensor_copy(blk_e[0:1, at:at + n], I[0:1, 0:n])
                v.tensor_copy(blk_row[0:1, at:at + n], I[0:1, P:P + n]).then_inc(s_blk, 1)
                dve.wait_ge(s_blk, part + 1)

            def expert_of(k):
                return dve.value_load(blk_e[0:1, bass.ds(k, 1)], min_val=0, max_val=E - 1)

            def copy_firsts(i, u):
                k = i * U + u
                e = expert_of(k)
                if not (isinstance(k, int) and k < R4):
                    apart(dve)
                    dve.wait_ge(s_gelu, k - (R4 - 1))
                v.tensor_copy(firsts_c[u % R4], firsts_sb[:, bass.ds(e * WB, WB2)]).then_inc(s_fc, 1)
                v.tensor_copy(b2c[u % U], firsts_sb[:, bass.ds(e * WB + WB2, D)]).then_inc(s_b2, 1)

            steps = [0]

            def batch(b, first=False, second=False, last=False, ahead=True):
                if not last:
                    normalise(b + 1, 0)
                v_values(b)
                q_low(b, 0)
                q_low(b, 1)
                if not first:
                    residual(b + -1)
                    second_stats(b + -1)
                if not last:
                    modulate(b + 1)
                if last:
                    early_counts()
                if not first and not second:
                    experts(b + -2)
                if last:
                    table(0)
                if not last:
                    hT_low(b + 1)
                kv_values(b, first)
                if not first:
                    normalise(b + -1, 1, first=second)
                if last:
                    table_rows(0)
                if not first and not second:
                    slots(b + -2)
                if last:
                    dve.wait_ge(s_w1, 16)
                    copy_firsts(0, 0)
                    copy_firsts(0, 1)
                if ahead:
                    first_stats(b + 2)
                attention(b)

            start, end = Batch(0, 0), Batch(0, B)
            first_stats(start + 1)
            dve.wait_ge(s_r, 16)
            over_batches(dve, batch)
            def result(i, u):
                k = i * U + u
                y, token = yb[u % U], ids[u % U]
                dve.wait_ge(s_y, k + 1)
                if not (isinstance(k, int) and k < U):
                    dve.wait_ge(s_yout[u % U], 16 * (i + u // U))
                dve.wait_ge(s_b2, k + 1)
                v.tensor_tensor(y, Y[u % 2][:, 0:D], b2c[u % U], ALU.add).then_inc(s_yst, 1)
                v.tensor_copy(token[:], xin[u % U][:, ID:ID + 1].bitcast(I32))
                dve.wait_ge(s_yst, 2 * k + 1)
                v.tensor_tensor(y, y, xin[u % U][:, GT:GT + D], ALU.mult).then_inc(s_yst, 1)
                if isinstance(k, int) and k < DVE_ADDS:
                    dve.wait_ge(s_yst, 2 * k + 2)
                    v.tensor_tensor(y, y, xin[u % U][:, X2:X2 + D], ALU.add).then_inc(s_yb, 1)

            def turn(i, first=False, last=False, between={}):
                for u in range(REST if last else U):
                    if not (last and u >= REST - 2):
                        copy_firsts(i, u + 2)
                    if not (first and u < 2):
                        result(i, u - 2)
                    for step in between.get(u, []):
                        step()

            turn(0, first=True, between={
                0: [lambda: experts(end + -2)],
                1: [lambda: slots(end + -2)],
                2: [lambda: residual(end + -1, bank=I)],
                3: [lambda: second_stats(end + -1)],
                4: [lambda: normalise(end + -1, 1)]})
            turn(1, between={
                3: [lambda: experts(end + -1)],
                4: [lambda: slots(end + -1)],
                5: [lambda: table(1)],
                7: [lambda: table_rows(1)]})
            with dve.Fori(2, TURNS - 1) as i:
                turn(i)
            turn(TURNS - 1, last=True)
            for u in range(2):
                result(TURNS - 1, REST - 2 + u)

        @block.tensor
        def _(pe):
            mm, tr = nc.tensor.matmul, nc.tensor.transpose

            pe.wait_ge(s_silu, 1)
            pe.wait_ge(s_wm, 16)
            sc = silu[:, 0, :]
            mm(KV[0:B, 0:3 * D], sc, wmod_sb[:, 0:3 * D], start=True, stop=True)
            mm(G[0:B, 0:3 * D], sc, wmod_sb[:, 3 * D:6 * D], start=True, stop=True)
            mm(F[0][:, 0:B], wmod_sb[:, 0:D], sc, start=True, stop=True)
            mm(F[0][:, B:2 * B], wmod_sb[:, D:2 * D], sc, start=True, stop=True).then_inc(s_modp, 1)

            def transpose_xn(b, first=False):
                pe.wait_ge(s_xn1, b.v + 1)
                if not first:
                    pe.wait_ge(s_x2, b.v - 1)
                for t in range(LT):
                    ins = tr(H[:, t * P:(t + 1) * P], xn1[:, t, :], ident)
                ins.then_inc(s_t1, 1)

            def project(b, i, first=False):
                if i == 0:
                    pe.wait_ge(s_hi, b.v + 1)
                    pe.wait_ge(s_lo, b.v + 1)
                    if not first:
                        pe.wait_ge(s_v, b.v)
                elif i == 1 and not first:
                    pe.wait_ge(s_qv, 2 * b.v)
                elif i in (2, 3):
                    pe.wait_ge(s_kval, 2 * b.v + i - 1)
                    pe.wait_ge(s_sq, 4 * b.v + i - 1)
                elif i == 4:
                    pe.wait_ge(s_qv, 2 * b.v + 1)
                if i < 4:
                    hi, lo = w_hi[:, i * P:(i + 1) * P], w_lo[:, i * P:(i + 1) * P]
                    mm(PJ[i % 2][:, :], hi, hT_hi[:], start=True, stop=False)
                    mm(PJ[i % 2][:, :], lo, hT_hi[:], start=False, stop=False)
                    mm(PJ[i % 2][:, :], hi, hT_lo[:], start=False, stop=True).then_inc(s_proj, 1)
                else:
                    for t in range(LT):
                        ins = mm(PJ[0][:, t * P:(t + 1) * P], hT[:, t * P:(t + 1) * P], wsb[:, W_V:W_V + D],
                                 start=True, stop=True)
                    ins.then_inc(s_proj, 1)

            def feature(b, j, first=False):
                if not (first and j < 2):
                    pe.wait_ge(s_exp, 2 * NC * b.v + j - 1)
                if j == 0:
                    pe.wait_ge(s_kval, 2 * b.v + 2)
                    pe.wait_ge(s_sq, 4 * b.v + 2)
                if j == LT:
                    pe.wait_ge(s_qlo, 2 * b.v + 2)
                ps = F[j % 2]
                if j < LT:
                    for half in range(2):
                        ins = mm(ps[:, half * 2 * P:(half + 1) * 2 * P], stack[half][:, j * P:(j + 1) * P],
                                 feat_w[:], start=True, stop=True)
                else:
                    c = j - LT
                    hi, lo = (w[:, (c % 2) * P:(c % 2 + 1) * P] for w in (fw_hi, fw_lo))
                    mm(ps[:, :], hi, q_hi[:, c // 2, :], start=True, stop=False)
                    mm(ps[:, :], lo, q_hi[:, c // 2, :], start=False, stop=False)
                    ins = mm(ps[:, :], hi, q_lo[:, c // 2, :], start=False, stop=True)
                ins.then_inc(s_feat, 1)

            def kv_product(b, first=False):
                pe.wait_ge(s_exp, 2 * NC * b.v + LT)
                pe.wait_ge(s_v, b.v + 1)
                if first:
                    pe.wait_ge(s_modr, 1)
                else:
                    pe.wait_ge(s_oT, b.v)
                for t in range(LT):
                    for c in range(NC):
                        mm(KV[c * CW:(c + 1) * CW, 0:P + 1], v_sb[:, t, c * CW:(c + 1) * CW], kf[:, t, c, 0:P + 1],
                           start=(t == 0), stop=(t == LT - 1))
                for t in range(LT):
                    for c in range(NC):
                        ins = mm(KV[c * CW:(c + 1) * CW, 256:256 + P], ones32[:], kf[:, t, c, 0:P],
                                 start=(t == 0), stop=(t == LT - 1))
                ins.then_inc(s_kv, 1)

            def kv_transpose(b):
                pe.wait_ge(s_kvT, b.v + 1)
                for n in range(2):
                    ins = tr(G[:, n * P:(n + 1) * P], kvT[:, n * P:(n + 1) * P], ident)
                ins.then_inc(s_kvt, 1)

            def attend(b):
                pe.wait_ge(s_kvm, b.v + 1)
                pe.wait_ge(s_exp, 2 * NC * (b.v + 1))
                for c in range(NC):
                    ins = mm(G[c * CW:(c + 1) * CW, :], kvm[:, P + c * CW:P + (c + 1) * CW], qf[:, c, :],
                             start=True, stop=True)
                ins.then_inc(s_den, 1)
                for c in range(NC):
                    ins = mm(KV[c * CW:(c + 1) * CW, :], kvm[:, c * CW:(c + 1) * CW], qf[:, c, :],
                             start=True, stop=True)
                ins.then_inc(s_num, 1)

            def out_project(b, last=False, bank=H):
                pe.wait_ge(s_oT, b.v + 1)
                pe.wait_ge(s_wo, b.v + 1)
                if last:
                    pe.wait_ge(s_slot, B - 1)
                else:
                    pe.wait_ge(s_hT, b.v + 2)
                for t in range(LT):
                    ins = mm(bank[:, t * P:(t + 1) * P], oT[:, t * P:(t + 1) * P], wo[:], start=True, stop=True)
                ins.then_inc(s_op, 1)

            def transpose_h2(b, first=False):
                pe.wait_ge(s_h2, b.v + 1)
                if not first:
                    pe.wait_ge(s_slot, b.v)
                for t in range(LT):
                    ins = tr(I[:, t * P:(t + 1) * P], pay[b.par][:, t, H2:H2 + D], ident)
                ins.then_inc(s_h2t, 1)

            def gate(b):
                pe.wait_ge(s_h2T, b.v + 1)
                for t in range(LT):
                    ins = mm(I[t * CW:(t + 1) * CW, 0:P], wsb[:, W_GATE:W_GATE + CW], h2T[:, t * P:(t + 1) * P],
                             start=True, stop=True)
                ins.then_inc(s_lg, 1)

            def gate_transpose(b):
                pe.wait_ge(s_lgT, b.v + 1)
                tr(I[:, P:2 * P], lgT[:], ident).then_inc(s_lgt, 1)

            def rank(b, first=False):
                pe.wait_ge(s_oh, b.v + 1)
                if not first:
                    pe.wait_ge(s_seen, b.v)
                out_ = I[:, 2 * P:2 * P + LT * E].rearrange("p (t e) -> p t e", t=LT)
                mm(out_, tri[:], oh[:], start=True, stop=False)
                for t in range(1, LT):
                    mm(out_[:, t:LT, :], ones_bf[:], oh[:, 0:LT - t, :], start=False, stop=False)
                mm(out_, ones_bf[:], seen[:, :].unsqueeze(1).to_broadcast([P, LT, E]), start=False, stop=True)\
                    .then_inc(s_rank, 1)

            def count(part):
                pe.wait_ge(s_seen, B if part else KNOWN)
                mm(I[:, 2 * P + LT * E:2 * P + LT * E + E], ones_bf[:], seen[:], start=True, stop=True)\
                    .then_inc(s_cnt, 1)

            def table_transpose(part):
                pe.wait_ge(s_tab, part + 1)
                for n in range(2):
                    ins = tr(I[0:1, n * P:(n + 1) * P], tab[:, n:n + 1], ident)
                ins.then_inc(s_tabT, 1)

            def batch(b, first=False, second=False, last=False, ahead=True):
                feature(b, 0, first)
                feature(b, 1, first)
                project(b, 4)
                if last:
                    pe.wait_ge(s_lgT, KNOWN + 1)
                    count(0)
                if not first and not second:
                    gate_transpose(b + -2)
                if not first:
                    out_project(b + -1)
                for j in range(2, LT + 2):
                    feature(b, j)
                if not last:
                    transpose_xn(b + 1, first)
                kv_product(b, first)
                if not first and not second:
                    rank(b + -2, first=isinstance(b.v, int) and b.v == 2)
                feature(b, LT + 2)
                feature(b, LT + 3)
                if last:
                    table_transpose(0)
                kv_transpose(b)
                if not last:
                    project(b + 1, 0)
                    project(b + 1, 1)
                attend(b)
                if not first:
                    transpose_h2(b + -1, first=second)
                if not last:
                    project(b + 1, 2)
                    project(b + 1, 3)
                if not first:
                    gate(b + -1)

            pe.wait_ge(s_fw, 3)
            pe.wait_ge(s_wlo, 2)
            pe.wait_ge(s_set, 4)
            start, end = Batch(0, 0), Batch(0, B)
            transpose_xn(start, first=True)
            for i in range(4):
                project(start, i, first=True)
            over_batches(pe, batch)

            pe.wait_ge(s_blk, 1)
            pe.wait_ge(s_w2, 16)

            def transpose_block(k, u, loads):
                pe.wait_ge(s_xin[u % U], 16 * loads)
                tr(XT[:, 0:P], xin[u % U][:, H2:H2 + D], ident).then_inc(s_bt, 1)

            def hidden(k, u):
                pe.wait_ge(s_fc, k + 1)
                pe.wait_ge(s_bT, k + 1)
                for c in range(FC):
                    ins = mm(HID[u % R4][:, c * P:(c + 1) * P], firsts_c[u % R4][:, c * P:(c + 1) * P], xT[u % 2][:],
                             start=True, stop=True)
                ins.then_inc(s_hid, 1)

            def second(k, u, early=False):
                e = pe.value_load(blk_e[0:1, bass.ds(k, 1)], min_val=0, max_val=E - 1)
                pe.wait_ge(s_gelu, k + 1)
                if not early:
                    pe.wait_ge(s_yst, 2 * k - 3)
                for c in range(FC):
                    ins = mm(Y[u % 2][:, 0:D], g[u % R4][:, c * P:(c + 1) * P], w2sb[:, bass.ds(e * DFF + c * D, D)],
                             start=(c == 0), stop=(c == FC - 1))
                ins.then_inc(s_y, 1)

            def turn(i, first=False, last=False, between={}):
                for u in range(REST if last else U):
                    k = i * U + u
                    if first and u == 2:
                        pe.wait_ge(s_oT, B)
                    hidden(k, u)
                    if not (last and u == REST - 1):
                        transpose_block(k + 1, u + 1, i + 1 + (u + 1) // U)
                    if not (first and u < 2):
                        second(k - 2, (u - 2) % U, early=first and u < 4)
                    if not (first or isinstance(i, int)) and u == U - 1:
                        pe.wait_ge(s_blk, 2)
                    for step in between.get(u, []):
                        step()

            transpose_block(0, 0, 1)
            turn(0, first=True, between={
                0: [lambda: gate_transpose(end + -2)],
                1: [lambda: rank(end + -2)],
                2: [lambda: out_project(end + -1, last=True, bank=I)]})
            turn(1, between={
                1: [lambda: transpose_h2(end + -1)],
                2: [lambda: gate(end + -1)],
                3: [lambda: gate_transpose(end + -1)],
                4: [lambda: rank(end + -1)],
                5: [lambda: count(1)],
                7: [lambda: table_transpose(1)]})
            with pe.Fori(2, TURNS - 1) as i:
                turn(i)
            turn(TURNS - 1, last=True)
            for u in range(2):
                second(NBLK - 2 + u, REST - 2 + u)


def program(nc, ins, outs):
    build(nc, *ins, *outs)


_OUT = (B, L, D)


def _constants():
    c = np.zeros((P, C_END), np.float32)
    p = np.arange(P)
    c[:, C_ID:C_ID + P] = np.eye(P)
    c[:, C_MASK:C_MASK + P] = (p[:, None] % CW) // DH == p[None, :] // M
    c[:, C_TRI:C_TRI + P] = p[:, None] < p[None, :]
    for r in range(64):
        head = r // DH
        c[64 + r, C_NORM + head * M:C_NORM + (head + 1) * M] = -1.0 / (2.0 * DH ** 0.5)
    c[:, C_PREF:C_PREF + E] = np.arange(E, 0, -1)
    c[:, C_LIST:C_LIST + E] = np.arange(E) * PITCH
    c[:, C_NUM:C_NUM + LT] = p[:, None] * LT + np.arange(LT)
    c[:, C_PAD] = NOROW + p
    c[:, C_P] = p
    return c


def kernel(L0_attn_x, L0_attn_Wq, L0_attn_bq, L0_attn_Wk, L0_attn_bk, L0_attn_Wv, L0_attn_bv, L0_attn_Wo,
           L0_attn_bo, L0_attn_orf, L0_ffn_gate_W, L0_ffn_gate_b, L0_ffn_W1, L0_ffn_b1, L0_ffn_W2, L0_ffn_b2,
           L0_c, L0_wmod):
    import concourse.bacc as bacc
    from concourse.bass_utils import run_bass_kernel_spmd

    a = lambda t: np.asarray(t)
    w = np.zeros((P, W_END), np.float32)
    wq, wk = a(L0_attn_Wq).T, a(L0_attn_Wk).T
    bq, bk = a(L0_attn_bq), a(L0_attn_bk)
    for n, (m, bias) in enumerate(((wk, bk), (wq, bq))):
        for half in range(2):
            cols, at = slice(64 * half, 64 * half + 64), (2 * n + half) * P
            w[:, at:at + 64] = m[:, cols]
            w[:, at + 64:at + P] = m[:, cols]
            w[0:64, W_BIAS + 2 * n + half] = bias[cols]
            w[64:, W_BIAS + 2 * n + half] = bias[cols]
    w[:, W_V:W_V + D] = a(L0_attn_Wv).T
    w[:, W_O:W_O + D] = a(L0_attn_Wo).T
    for head in range(64 // DH):
        w[head * DH:(head + 1) * DH, W_ORF + head * M:W_ORF + (head + 1) * M] = a(L0_attn_orf).T
    w[:, W_GATE:W_GATE + E] = a(L0_ffn_gate_W)
    w[:, W_CT:W_CT + B] = a(L0_c).T
    rows = np.concatenate([a(L0_attn_bv), a(L0_attn_bo), a(L0_ffn_gate_b)])
    rows = np.ascontiguousarray(np.broadcast_to(rows, (P, R_END)))

    firsts = np.zeros((P, E, WB), np.float32)
    firsts[:, :, 0:DFF] = a(L0_ffn_W1).transpose(1, 0, 2)
    firsts[:, :, WB2:WB] = a(L0_ffn_b2)
    firsts[:, :, WB1:WB2] = a(L0_ffn_b1).reshape(E, FC, P).transpose(2, 0, 1)

    ins = {"x": a(L0_attn_x), "weights": w, "consts": _constants(), "rows": rows, "wmod": a(L0_wmod),
           "firsts": firsts.reshape(P, E * WB),
           "w2": a(L0_ffn_W2)}
    nc = bacc.Bacc("TRN2", target_bir_lowering=False, num_devices=1)
    arrays = {f"in_{n}": np.ascontiguousarray(v) for n, v in ins.items()}
    aps = [nc.dram_tensor(n, v.shape, mybir.dt.from_np(v.dtype), kind="ExternalInput").ap()
           for n, v in arrays.items()]
    out = nc.dram_tensor("out", _OUT, F32, kind="ExternalOutput").ap()
    program(nc, aps, [out])
    r = run_bass_kernel_spmd(nc, [arrays], core_ids=[0])
    return r.results[0]["out"]
```
